# Optimizing a Trainium2 kernel written in Bass

```python
import numpy as np
import jax
import jax.numpy as jnp

def _softmax(x, axis=-1):
    return jax.nn.softmax(x, axis=axis)

def _gelu(x):
    return jax.nn.gelu(x, approximate=True)

def _silu(x):
    return jax.nn.silu(x)

def _sigmoid(x):
    return jax.nn.sigmoid(x)

def _layernorm(x, axis=-1, eps=1e-05):
    m = jnp.mean(x, axis=axis, keepdims=True)
    v = jnp.var(x, axis=axis, keepdims=True)
    return (x - m) / jnp.sqrt(v + eps)

def _scatter_add(tgt, idx, src, axis=0):
    return tgt.at[idx].add(src)

def _segment_sum(src, seg, n):
    return jax.ops.segment_sum(src, seg, n)
kernel_name = 'mk_cond_resid_d4_seqx_r4_cccbc9'

def setup_inputs(seed: int=0):
    np.random.seed(seed)
    _w = jnp.asarray

    def _rec_inputs():
        import jax
        import jax.numpy as jnp
        _rk = jax.random.key(seed)
        x = 8.748e-05 + 1 * jax.random.normal(jax.random.fold_in(_rk, 1), (4, 512, 512), jnp.float32)
        _lenS = 512 - jax.random.randint(jax.random.fold_in(_rk, 7), (4,), 0, max(1, 512 // 4) + 1, jnp.int32)
        _lenS2 = 512 - jax.random.randint(jax.random.fold_in(_rk, 8), (4,), 0, max(1, 512 // 4) + 1, jnp.int32)
        fside_BxSx1_0 = -0.00499425 + 1.0058 * jax.random.normal(jax.random.fold_in(_rk, 11), (4, 512, 1), jnp.float32)
        cond_2048 = 0.00513981 + 1.0024 * jax.random.normal(jax.random.fold_in(_rk, 12), (4, 512), jnp.float32)
        return (x, fside_BxSx1_0, cond_2048)
    x, fside_BxSx1_0, cond_2048 = _rec_inputs()

    def _L0_cond_setup():
        import jax, jax.numpy as jnp
        import numpy as np
        G, N, K = (16, 512, 5120)
        key = jax.random.key(seed)
        k1, k2, k3 = jax.random.split(key, 3)
        return {'emb_s': jax.random.normal(k1, (G, N, 1), dtype=jnp.float32), 'emb_t': jax.random.normal(k2, (G, 1, N), dtype=jnp.float32), 'attention_weights': jax.random.normal(k3, (G, N, N), dtype=jnp.float32), 'k': K}
    _L0_cond_all = _L0_cond_setup()
    _L0_cond_in = {k: v for k, v in _L0_cond_all.items() if k in ()}
    del _L0_cond_all

    def _L1_cond_setup():
        import jax, jax.numpy as jnp
        import numpy as np
        HEADS = 16
        EPS = 1e-06

        def _rms_norm(x, g):
            xf = x.astype(jnp.float32)
            y = xf * jax.lax.rsqrt(jnp.mean(xf * xf, axis=-1, keepdims=True) + EPS)
            return y.astype(x.dtype) * g
        key = jax.random.key(seed)
        ks = jax.random.split(key, 6)
        b, n, dim, emb_dim = (4, 512, 512, 512)
        d_head = dim // HEADS
        return {'x': jax.random.normal(ks[0], (b, n, dim), jnp.float32), 'emb': jax.random.normal(ks[1], (b, 1, emb_dim), jnp.float32), 'W_emb': jax.random.normal(ks[2], (emb_dim, 2 * dim), jnp.float32) * emb_dim ** (-0.5), 'b_emb': jnp.zeros((2 * dim,), jnp.float32), 'g_norm': jnp.ones((dim,), jnp.float32), 'W_qkv': jax.random.normal(ks[3], (dim, 3 * dim), jnp.float32) * dim ** (-0.5), 'g_q': jnp.ones((d_head,), jnp.float32), 'g_k': jnp.ones((d_head,), jnp.float32), 'W_out': jax.random.normal(ks[4], (dim, dim), jnp.float32) * dim ** (-0.5)}
    _L1_cond_all = _L1_cond_setup()
    _L1_cond_in = {k: v for k, v in _L1_cond_all.items() if k in ('W_emb', 'b_emb', 'g_norm', 'W_qkv', 'g_q', 'g_k', 'W_out')}
    del _L1_cond_all

    def _L2_cond_setup():
        import jax, jax.numpy as jnp
        import numpy as np
        B, T, D = (16, 128, 512)
        key = jax.random.key(seed)
        k0, k1, k2, k3 = jax.random.split(key, 4)
        scale = 1.0 / np.sqrt(D)
        return {'initial_state': jax.random.normal(k0, (B, D), jnp.float32), 'inputs': jax.random.normal(k1, (B, T, D), jnp.float32), 'W_ih': jax.random.normal(k2, (D, 3 * D), jnp.float32) * scale, 'W_hh': jax.random.normal(k3, (D, 3 * D), jnp.float32) * scale, 'b_ih': jnp.zeros((3 * D,), jnp.float32), 'b_hh': jnp.zeros((3 * D,), jnp.float32)}
    _L2_cond_all = _L2_cond_setup()
    _L2_cond_in = {k: v for k, v in _L2_cond_all.items() if k in ('W_ih', 'W_hh', 'b_ih', 'b_hh')}
    del _L2_cond_all

    def _L3_cond_setup():
        import jax, jax.numpy as jnp
        import numpy as np
        N, C, L_IN, L_OUT = (32, 64, 512, 512)
        key = jax.random.key(seed)
        k1, k2 = jax.random.split(key)
        inp = jax.random.normal(k1, (N, C, L_IN), dtype=jnp.float32)
        grid = jax.random.uniform(k2, (N, L_OUT), dtype=jnp.float32) * 2.0 - 1.0
        return {'input': inp, 'grid': grid, 'padding_mode': 1, 'align_corners': 1}
    _L3_cond_all = _L3_cond_setup()
    _L3_cond_in = {k: v for k, v in _L3_cond_all.items() if k in ()}
    del _L3_cond_all
    return {'x': x, 'fside_BxSx1_0': fside_BxSx1_0, 'cond_2048': cond_2048, 'L1_cond_W_emb': _L1_cond_in['W_emb'], 'L1_cond_b_emb': _L1_cond_in['b_emb'], 'L1_cond_g_norm': _L1_cond_in['g_norm'], 'L1_cond_W_qkv': _L1_cond_in['W_qkv'], 'L1_cond_g_q': _L1_cond_in['g_q'], 'L1_cond_g_k': _L1_cond_in['g_k'], 'L1_cond_W_out': _L1_cond_in['W_out'], 'L2_cond_W_ih': _L2_cond_in['W_ih'], 'L2_cond_W_hh': _L2_cond_in['W_hh'], 'L2_cond_b_ih': _L2_cond_in['b_ih'], 'L2_cond_b_hh': _L2_cond_in['b_hh']}

def reference(x, fside_BxSx1_0, cond_2048, L1_cond_W_emb, L1_cond_b_emb, L1_cond_g_norm, L1_cond_W_qkv, L1_cond_g_q, L1_cond_g_k, L1_cond_W_out, L2_cond_W_ih, L2_cond_W_hh, L2_cond_b_ih, L2_cond_b_hh):
    import jax
    import jax.numpy as jnp

    def _L0_cond_ref(emb_s, emb_t, attention_weights, k):
        import jax, jax.numpy as jnp
        import numpy as np
        G, N, K = (16, 512, 5120)
        g, n = (emb_s.shape[0], emb_s.shape[1])
        adj = emb_s * emb_t
        att = jax.nn.softmax(attention_weights, axis=-1) * (1.0 / np.sqrt(n).astype(np.float32))
        adj = adj * att
        diag = jnp.arange(n)
        adj = adj.at[:, diag, diag].set(-jnp.inf)
        flat = adj.reshape(g, n * n)
        _, idx = jax.lax.top_k(flat, k)
        rows = jnp.arange(g)[:, None]
        out = jnp.zeros((g, n * n), dtype=adj.dtype).at[rows, idx].set(1.0)
        return out.reshape(g, n, n)

    def _L1_cond_ref(x, emb, W_emb, b_emb, g_norm, W_qkv, g_q, g_k, W_out):
        import jax, jax.numpy as jnp
        import numpy as np
        HEADS = 16
        EPS = 1e-06

        def _rms_norm(x, g):
            xf = x.astype(jnp.float32)
            y = xf * jax.lax.rsqrt(jnp.mean(xf * xf, axis=-1, keepdims=True) + EPS)
            return y.astype(x.dtype) * g
        b, n, dim = x.shape
        h = HEADS
        d = dim // h
        scale_shift = emb @ W_emb + b_emb
        scale, shift = jnp.split(scale_shift, 2, axis=-1)
        xn = _rms_norm(x, g_norm) * (1.0 + scale) + shift
        qkv = xn @ W_qkv
        qkv = qkv.reshape(b, n, 3, h, d)
        q, k, v = jnp.moveaxis(qkv, 2, 0)
        q = jnp.swapaxes(q, 1, 2)
        k = jnp.swapaxes(k, 1, 2)
        v = jnp.swapaxes(v, 1, 2)
        q = _rms_norm(q, g_q)
        k = _rms_norm(k, g_k)
        logits = jnp.einsum('bhqd,bhkd->bhqk', q, k) * d ** (-0.5)
        attn = jax.nn.softmax(logits, axis=-1)
        o = jnp.einsum('bhqk,bhkd->bhqd', attn, v)
        o = jnp.swapaxes(o, 1, 2).reshape(b, n, dim)
        return o + o @ W_out

    def _L2_cond_ref(initial_state, inputs, W_ih, W_hh, b_ih, b_hh):
        import jax, jax.numpy as jnp
        import numpy as np
        B, T, D = (16, 128, 512)
        "ScanOverTime(GRU cell): sequential per-timestep module call with\n            dict-state passing; merge_dict_trees stacks the per-step\n            'state_predicted' tensors along axis=1 -> [B, T, D]."

        def cell(h, x):
            gi = x @ W_ih + b_ih
            gh = h @ W_hh + b_hh
            i_r, i_z, i_n = jnp.split(gi, 3, axis=-1)
            h_r, h_z, h_n = jnp.split(gh, 3, axis=-1)
            r = jax.nn.sigmoid(i_r + h_r)
            z = jax.nn.sigmoid(i_z + h_z)
            n = jnp.tanh(i_n + r * h_n)
            h_new = (1.0 - z) * n + z * h
            return (h_new, h_new)
        xs = jnp.swapaxes(inputs, 0, 1)
        _, hs = jax.lax.scan(cell, initial_state, xs)
        return jnp.swapaxes(hs, 0, 1)

    def _L3_cond_ref(input, grid, padding_mode, align_corners):
        import jax, jax.numpy as jnp
        import numpy as np
        N, C, L_IN, L_OUT = (32, 64, 512, 512)
        L = input.shape[2]
        if align_corners:
            ix = (grid + 1.0) * 0.5 * (L - 1)
        else:
            ix = ((grid + 1.0) * L - 1.0) * 0.5
        x0 = jnp.floor(ix)
        w1 = ix - x0
        w0 = 1.0 - w1
        i0 = x0.astype(jnp.int32)
        i1 = i0 + 1
        i0c = jnp.clip(i0, 0, L - 1)
        i1c = jnp.clip(i1, 0, L - 1)
        v0 = jnp.take_along_axis(input, i0c[:, None, :], axis=2)
        v1 = jnp.take_along_axis(input, i1c[:, None, :], axis=2)
        if padding_mode:
            return w0[:, None, :] * v0 + w1[:, None, :] * v1
        else:
            m0 = ((i0 >= 0) & (i0 < L)).astype(input.dtype)
            m1 = ((i1 >= 0) & (i1 < L)).astype(input.dtype)
            return (w0 * m0)[:, None, :] * v0 + (w1 * m1)[:, None, :] * v1
    x = x + _L0_cond_ref(fside_BxSx1_0, cond_2048[:, None, :], x, 5120)
    x = x + _L1_cond_ref(x, cond_2048[:, None, :], L1_cond_W_emb, L1_cond_b_emb, L1_cond_g_norm, L1_cond_W_qkv, L1_cond_g_q, L1_cond_g_k, L1_cond_W_out)
    x = x + _L2_cond_ref(cond_2048, x, L2_cond_W_ih, L2_cond_W_hh, L2_cond_b_ih, L2_cond_b_hh)
    x = x + _L3_cond_ref(x, cond_2048, 1, 1)
    return x

_drawn_inputs = setup_inputs


def setup_inputs(seed=0):
    import zlib

    import numpy as np

    out = dict(_drawn_inputs(seed))
    spreads = {'L1_cond_b_emb': (0.0, 0.1),
     'L1_cond_g_norm': (1.0, 0.2),
     'L1_cond_g_q': (1.0, 0.6),
     'L1_cond_g_k': (1.0, 0.6),
     'L2_cond_b_ih': (0.0, 0.314),
     'L2_cond_b_hh': (0.0, 0.461)}
    factors = {}
    for name, (base, spread) in spreads.items():
        noise = np.random.default_rng([zlib.crc32(name.encode()), seed]).standard_normal(out[name].shape)
        drawn = base * np.exp(spread * noise) if base else spread * noise
        out[name] = jnp.asarray(drawn.astype(out[name].dtype))
    for name, factor in factors.items():
        out[name] = (out[name] * factor).astype(out[name].dtype)
    return out
```

```python
from contextlib import ExitStack

import concourse.bass as bass
from concourse import mybir
from concourse.alu_op_type import AluOpType as ALU

FP32 = mybir.dt.float32
FP16 = mybir.dt.float16
INT32 = mybir.dt.int32
INT16 = mybir.dt.int16
UINT16 = mybir.dt.uint16
ACT = mybir.ActivationFunctionType
AX = mybir.AxisListType

P = 128
B, S, D = 4, 512, 512
NT = S // P
NC = D // P
TOPK = 5120
HEADS = 16
DH = D // HEADS
HPG = P // DH
GATES = 3
EPS = 1e-6
LOWEST = -3.0e38


class Program:

    ENGINES = {"pe": "tensor", "dve": "vector", "act": "scalar", "pool": "gpsimd", "sp": "sync"}

    def __init__(self, nc, ctx):
        self.nc, self.ctx = nc, ctx
        self.queues = {e: [] for e in self.ENGINES}
        self.semaphores, self.counts, self.waited = {}, {}, {}

    def add(self, engine, emit, wait=(), done=None, by=1):
        waits = []
        for event in wait:
            if event is not None and self.waited.get((engine, event[0]), 0) < event[1]:
                self.waited[engine, event[0]] = event[1]
                waits.append(event)
        if done is not None:
            if done not in self.semaphores:
                self.semaphores[done] = self.ctx.enter_context(self.nc.semaphore(done))
                self.counts[done] = 0
            self.counts[done] += by
        made = None if done is None else (done, self.counts[done])

        def run(eng):
            for name, value in waits:
                eng.wait_ge(self.semaphores[name], value)
            instruction = emit(eng) if emit is not None else None
            if made is not None:
                instruction.then_inc(self.semaphores[done], by)

        self.queues[engine].append(run)
        return made

    def dma(self, engine, out, in_, done, wait=(), by_element=False):
        return self.add(engine, lambda e: e.dma_start(out, in_, allow_slow_non_contiguous=by_element), wait, done, 16)

    def emit(self):
        with self.nc.Block() as block:
            for name, attribute in self.ENGINES.items():
                def run(eng, name=name):
                    for item in self.queues[name]:
                        item(eng)
                {"tensor": block.tensor, "vector": block.vector, "scalar": block.scalar,
                 "gpsimd": block.gpsimd, "sync": block.sync}[attribute](run)


class Memory:

    def __init__(self, nc, ctx):
        self.nc, self.ctx = nc, ctx
        self.banks = [ctx.enter_context(nc.psum_tensor(f"bank{i}", [P, 512], FP32)) for i in range(8)]
        kib = {"rows": 32, "cols": 32, "work": 32.25, "cond": 8, "w_a": 24, "w_out": 8, "w_b": 24,
               "w_hh": 24, "scratch": 16}
        self.regions = {n: ctx.enter_context(nc.sbuf_tensor(f"region_{n}", [P, int(k * 256)], FP32))
                        for n, k in kib.items()}

    def view(self, region, at_kib, dtype, *shape):
        n = 1
        for s in shape:
            n *= s
        words = n * {FP32: 4, INT32: 4, FP16: 2, INT16: 2, UINT16: 2}[dtype] // 4
        flat = self.regions[region][:, int(at_kib * 256):int(at_kib * 256) + words]
        if dtype is not FP32:
            flat = flat.bitcast(dtype)
        names = " ".join(f"d{i}" for i in range(len(shape)))
        sizes = {f"d{i}": s for i, s in enumerate(shape[1:], 1)}
        return flat.rearrange(f"p ({names}) -> p {names}", **sizes) if len(shape) > 1 else flat

    def small(self, name, *shape, dtype=FP32):
        return self.ctx.enter_context(self.nc.sbuf_tensor(name, [P, *shape], dtype))

    def bank(self, i, *shape, at=0):
        n = 1
        for s in shape:
            n *= s
        names = " ".join(f"d{j}" for j in range(len(shape)))
        sizes = {f"d{j}": s for j, s in enumerate(shape[1:], 1)}
        flat = self.banks[i][:, at:at + n]
        return flat.rearrange(f"p ({names}) -> p {names}", **sizes) if len(shape) > 1 else flat


def build(nc, x, fside, cond, w_emb, b_emb, g_norm, w_qkv, g_q, g_k, w_out, w_ih, w_hh, b_ih, b_hh, out,
          debug=None):
    with ExitStack() as ctx:
        pr = Program(nc, ctx)
        mem = Memory(nc, ctx)
        c = constants(pr, mem)
        load(pr, mem, c, x, fside, cond, w_emb, b_emb, g_norm, w_qkv, g_q, g_k, w_out, w_ih, w_hh, b_ih, b_hh)
        scales(pr, mem, c)
        top_k(pr, mem, c)
        if debug == "mask":
            for b in range(B):
                dump(pr, out, c.x[:, b], b, c)
            pr.emit()
            return
        attention(pr, mem, c, w_ih, cond)
        if debug == "attn":
            dump_cols(pr, out, c.xT, c)
            pr.emit()
            return
        floor_and_weights(pr, mem, c, cond)
        left = gru(pr, mem, c, cond, out)
        last_tile(pr, mem, c, left, out)
        pr.emit()


def dump(pr, out, src, b, c):
    e = pr.dma("sp", out[b].rearrange("(t p) d -> p t d", p=P), src, f"dump{b}", wait=[c.x1[b]])
    pr.add("sp", None, wait=[e])


def dump_cols(pr, out, xT, c):
    for b in range(B):
        e = pr.dma("sp", out[b].rearrange("(p k) s -> p k s", k=NC), xT[:, :, b, :], f"dumpc", wait=c.x2)
    pr.add("sp", None, wait=[e])


class Names:
    pass


def constants(pr, mem):
    c = Names()
    c.ident = mem.small("ident", P)
    c.ident16 = mem.small("ident16", P, dtype=FP16)
    c.ones = mem.small("ones", P)
    c.minus_halves = mem.view("cols", 25, FP32, P)
    c.before = mem.view("cols", 25.5, FP32, P)
    c.feature = mem.small("feature", NC)
    pr.add("pool", lambda e: e.memset(c.ident[:], 0.0), done="const0")
    pr.add("pool", lambda e: e.memset(c.ident16[:], 0.0), done="const0")
    pr.add("pool", lambda e: e.memset(c.ones[:], 1.0), done="const0")
    z = pr.add("pool", lambda e: e.memset(c.minus_halves, -0.5), done="const0")
    for m in (c.ident, c.ident16):
        pr.add("pool", lambda e, m=m: e.affine_select(out=m[:], in_=m[:], compare_op=ALU.not_equal, fill=1.0,
                                                     base=0, pattern=[[-1, P]], channel_multiplier=1),
               wait=[z], done="const")
    pr.add("pool", lambda e: e.affine_select(out=c.before, in_=c.ones[:], compare_op=ALU.is_gt, fill=0.0,
                                             base=0, pattern=[[1, P]], channel_multiplier=-1), wait=[z], done="const")
    c.const = pr.add("pool", lambda e: e.iota(c.feature[:], [[P, NC]], base=0, channel_multiplier=1,
                                              allow_small_or_imprecise_dtypes=True), done="const")
    return c


def load(pr, mem, c, x, fside, cond, w_emb, b_emb, g_norm, w_qkv, g_q, g_k, w_out, w_ih, w_hh, b_ih, b_hh):
    c.x = mem.view("rows", 0, FP32, B, NT, D)
    c.cond_rows = mem.view("cond", 0, FP32, B, D)
    c.fside = mem.small("fside", B, NT)
    c.condT = mem.small("condT", B, NC)
    c.b_emb = mem.small("b_emb", 2 * NC)
    c.g_norm = mem.small("g_norm", NC)
    c.g_q = mem.small("g_q", DH)
    c.g_k = mem.small("g_k", DH)
    c.b_ih = mem.small("b_ih", GATES, NC)
    c.b_hh = mem.small("b_hh", GATES, NC)
    c.w_hh_raw = [mem.view(region, at, FP32, GATES * D) for region, at in
                  (("scratch", 0), ("scratch", 6), ("cols", 26), ("w_b", 18))]
    c.w_emb = mem.view("cols", 0, FP32, NC, 2 * D)
    c.w_qkv = mem.view("w_a", 0, FP32, NC, GATES * D)
    c.w_out = mem.view("w_out", 0, FP32, NC, D)
    c.x_in = [None] * B
    c.x_in[0] = pr.dma("sp", c.x[:, 0], x[0].rearrange("(t p) d -> p t d", p=P), "x_in0")
    c.cond_in = pr.dma("act", c.cond_rows.rearrange("p b d -> p (b d)"),
                       cond.rearrange("b d -> (b d)").partition_broadcast(P), "cond_in")
    for b in range(B):
        c.fside_in = pr.dma("act", c.fside[:, b], fside[b].rearrange("(t p) o -> p (t o)", p=P), "fside_in", by_element=True)
    for b in range(1, B):
        c.x_in[b] = pr.dma("sp", c.x[:, b], x[b].rearrange("(t p) d -> p t d", p=P), f"x_in{b}")
    for b in range(B):
        pr.dma("sp", c.condT[:, b], cond[b].rearrange("(k p) -> p k", p=P), "small_in", by_element=True)
    pr.dma("sp", c.b_emb[:], b_emb.rearrange("(k p) -> p k", p=P), "small_in", by_element=True)
    pr.dma("sp", c.g_norm[:], g_norm.rearrange("(k p) -> p k", p=P), "small_in", by_element=True)
    pr.dma("sp", c.g_q[:], g_q.partition_broadcast(P), "small_in")
    pr.dma("sp", c.g_k[:], g_k.partition_broadcast(P), "small_in")
    pr.dma("sp", c.b_ih[:], b_ih.rearrange("(g k p) -> p g k", p=P, k=NC), "small_in", by_element=True)
    c.small_in = pr.dma("sp", c.b_hh[:], b_hh.rearrange("(g k p) -> p g k", p=P, k=NC), "small_in", by_element=True)
    for k in range(NC):
        c.w_hh_in = pr.dma("sp", c.w_hh_raw[k], w_hh[k * P:(k + 1) * P], "w_hh_in")
    c.w_emb_in = pr.dma("sp", c.w_emb, w_emb.rearrange("(k p) n -> p k n", p=P), "w_emb_in")
    c.w_qkv_in = pr.dma("sp", c.w_qkv, w_qkv.rearrange("(k p) n -> p k n", p=P), "w_qkv_in")
    c.w_out_in = pr.dma("sp", c.w_out, w_out.rearrange("(k p) n -> p k n", p=P), "w_out_in")


def power_of_two(pr, name, dst, src, wait):
    return pr.add("dve", lambda e: e.tensor_scalar(dst.bitcast(INT32), src.bitcast(INT32), 0x7F800000, None,
                                                   ALU.bitwise_and), wait=wait, done=name)


def scales(pr, mem, c):
    chunk_most = mem.small("chunk_most", NC)
    most = mem.small("most", 3)
    absmax = mem.small("absmax", 3)
    c.gain = mem.small("gain", DH)
    gains = pr.add("dve", lambda e: e.tensor_tensor(c.gain[:], c.g_q[:], c.g_k[:], ALU.mult),
                   wait=[c.small_in], done="prepared")
    pr.add("dve", lambda e: e.tensor_reduce(most[:, 2:3], c.gain[:], AX.X, ALU.max, apply_absolute_value=True),
           wait=[gains], done="prepared")
    pr.add("dve", lambda e: e.tensor_reduce(most[:, 1:2], c.condT[:].rearrange("p b k -> p (b k)"), AX.X, ALU.max,
                                            apply_absolute_value=True), done="prepared")
    for k in range(NC):
        m = pr.add("dve", lambda e, k=k: e.tensor_reduce(chunk_most[:, k:k + 1], c.w_hh_raw[k], AX.X, ALU.max,
                                                         apply_absolute_value=True), wait=[c.w_hh_in], done="prepared")
    m = pr.add("dve", lambda e: e.tensor_reduce(most[:, 0:1], chunk_most[:], AX.X, ALU.max), wait=[m], done="prepared")
    r = pr.add("pool", lambda e: e.partition_all_reduce(absmax[:], most[:], P, bass.bass_isa.ReduceOp.max),
               wait=[m], done="absmax")
    guarded = mem.small("guarded", 3)
    pr.add("dve", lambda e: e.tensor_scalar(guarded[:, 0:3:2], absmax[:, 0:3:2], 2.0 ** -60, None, ALU.max),
           wait=[r], done="prepared")
    g = pr.add("dve", lambda e: e.tensor_scalar(guarded[:, 1:2], absmax[:, 1:2], 1.0, None, ALU.max), done="prepared")
    power = mem.small("power", 3)
    p = power_of_two(pr, "prepared", power[:], guarded[:], [g])
    inverse = mem.small("inverse", 3)
    i = pr.add("dve", lambda e: e.reciprocal(inverse[:], power[:]), wait=[p], done="prepared")
    c.w_scale = mem.small("w_scale", 1)
    c.h_scale = mem.small("h_scale", 1)
    c.h_unscale = mem.small("h_unscale", 1)
    c.gate_scale = mem.small("gate_scale", 1)
    c.gate_unscale = mem.small("gate_unscale", 1)
    c.minus_h_scale = mem.small("minus_h_scale", 1)
    pr.add("dve", lambda e: e.tensor_scalar(c.w_scale[:], inverse[:, 0:1], 2.0 ** 13, None, ALU.mult), wait=[i], done="prepared")
    pr.add("dve", lambda e: e.tensor_scalar(c.minus_h_scale[:], inverse[:, 1:2], -2.0 ** 12, None, ALU.mult), done="prepared")
    pr.add("dve", lambda e: e.tensor_scalar(c.h_unscale[:], power[:, 1:2], 2.0 ** -12, None, ALU.mult), done="prepared")
    s0 = pr.add("dve", lambda e: e.tensor_scalar(c.h_scale[:], inverse[:, 1:2], 2.0 ** 12, None, ALU.mult), done="prepared")
    pr.add("dve", lambda e: e.tensor_scalar(c.gate_scale[:], c.w_scale[:], c.h_scale[:], None, ALU.mult), wait=[s0], done="prepared")
    s1 = pr.add("dve", lambda e: e.tensor_scalar(c.gate_unscale[:], power[:, 0:1], 2.0 ** -13, None, ALU.mult), done="prepared")
    c.scale = pr.add("dve", lambda e: e.tensor_scalar(c.gate_unscale[:], c.gate_unscale[:], c.h_unscale[:], None, ALU.mult),
                     wait=[s1], done="prepared")
    c.logit_scale = mem.small("logit_scale", 1)
    c.minus_logit_scale = mem.small("minus_logit_scale", 1)
    pr.add("dve", lambda e: e.tensor_scalar(c.gain[:], c.gain[:], inverse[:, 2:3], None, ALU.mult), wait=[i, gains], done="prepared")
    pr.add("dve", lambda e: e.tensor_scalar(c.minus_logit_scale[:], power[:, 2:3], -float(DH) ** -0.5, None, ALU.mult), done="prepared")
    c.gain_done = pr.add("dve", lambda e: e.tensor_scalar(c.logit_scale[:], power[:, 2:3], float(DH) ** -0.5, None, ALU.mult),
                         done="prepared")

    c.w16 = mem.view("w_hh", 0, FP16, 2, NC, 2 * GATES * 2, P)
    for k in range(NC):
        raw = c.w_hh_raw[k]
        scaled = pr.add("act", lambda e, raw=raw: e.activation(raw, raw, ACT.Copy, scale=c.w_scale[:]),
                        wait=[c.scale], done="w_scaled")
        for g in range(GATES):
            src = raw[:, g * D:(g + 1) * D].rearrange("p (m c n) -> p m c n", m=2, c=2)
            parts = [c.w16[:, part, k].rearrange("p (m g c) n -> p m g c n", m=2, g=GATES)[:, :, g] for part in range(2)]
            hi = pr.add("act", lambda e, src=src, parts=parts: e.activation(parts[0], src, ACT.Copy),
                        wait=[scaled], done="w_high")
            c.w16_done = pr.add("pool", lambda e, src=src, parts=parts: e.tensor_tensor(parts[1], src, parts[0], ALU.subtract),
                                wait=[hi, scaled], done="w_low")

    ss = mem.bank(7, 2 * NC, B)
    for j in range(2 * NC):
        for k in range(NC):
            e1 = pr.add("pe", lambda e, j=j, k=k: e.matmul(ss[:, j], c.w_emb[:, k, j * P:(j + 1) * P], c.condT[:, :, k],
                                                           start=(k == 0), stop=(k == NC - 1)),
                        wait=[c.w_emb_in, c.small_in], done="emb" if j == 2 * NC - 1 and k == NC - 1 else None)
    c.w_emb_read = e1
    emb = mem.small("emb", 2 * NC, B)
    c.col_scale = mem.small("col_scale", NC, B)
    c.col_shift = emb[:, NC:]
    e2 = pr.add("dve", lambda e: e.tensor_tensor(emb[:], ss, c.b_emb[:].unsqueeze(2).broadcast_to([P, 2 * NC, B]), ALU.add),
                wait=[e1, c.small_in], done="prepared")
    c.emb_read = e2
    e3 = pr.add("dve", lambda e: e.tensor_scalar(c.col_scale[:], emb[:, :NC], 1.0, None, ALU.add), wait=[e2], done="prepared")
    c.col_done = pr.add("dve", lambda e: e.tensor_tensor(c.col_scale[:], c.col_scale[:],
                                                        c.g_norm[:].unsqueeze(2).broadcast_to([P, NC, B]), ALU.mult),
                        wait=[e3], done="prepared")


def top_k(pr, mem, c):
    v = mem.view("work", 0, FP32, B, NT, D)
    neg_max, total = mem.small("neg_max", B, NT), mem.small("total", B, NT)
    row_scale = mem.small("row_scale", B, NT)
    value = [None] * B
    for b in range(B):
        m = pr.add("dve", lambda e, b=b: e.tensor_reduce(neg_max[:, b], c.x[:, b], AX.X, ALU.max, negate=True),
                   wait=[c.x_in[b]], done="weighted")
        for t in range(NT):
            ex = pr.add("act", lambda e, b=b, t=t: e.activation(v[:, b, t], c.x[:, b, t], ACT.Exp, bias=neg_max[:, b, t:t + 1],
                                                                accum_out=total[:, b, t:t + 1]), wait=[m], done="exp_rows")
        r = pr.add("dve", lambda e, b=b: e.reciprocal(row_scale[:, b], total[:, b]), wait=[ex], done="weighted")
        r = pr.add("dve", lambda e, b=b: e.scalar_tensor_tensor(row_scale[:, b], row_scale[:, b], float(S) ** -0.5, c.fside[:, b],
                                                                ALU.mult, ALU.mult), wait=[r, c.fside_in], done="weighted")
        for t in range(NT):
            w = pr.add("dve", lambda e, b=b, t=t: e.scalar_tensor_tensor(v[:, b, t], v[:, b, t], row_scale[:, b, t:t + 1],
                                                                         c.cond_rows[:, b], ALU.mult, ALU.mult),
                       wait=[r, c.cond_in], done="weighted")
            value[b] = pr.add("pool", lambda e, b=b, t=t: e.affine_select(
                out=v[:, b, t, t * P:(t + 1) * P], in_=v[:, b, t, t * P:(t + 1) * P], compare_op=ALU.not_equal,
                fill=LOWEST, base=0, pattern=[[-1, P]], channel_multiplier=1), wait=[w, c.const], done="diagonal")

    c.cond_read = [w]
    N = S * D
    PER = NT * D
    flat = [v[:, b].rearrange("p t d -> p (t d)") for b in range(B)]
    keys = mem.view("w_b", 0, INT16, B, PER)
    lows = mem.view("w_b", 0, UINT16, B, PER)
    junk = mem.view("cols", 16, INT16, PER)
    junk_act = mem.view("cols", 20, INT16, PER)
    tally = mem.small("tally", B)
    tally_act = mem.small("tally_act", B)
    sign = mem.small("sign", B)
    rank = mem.small("rank", B)
    for b in range(B):
        t0 = pr.add("dve", lambda e, b=b: e.tensor_scalar(junk, flat[b], 0.0, 0.0, ALU.is_ge, ALU.add,
                                                          accum_out=tally[:, b:b + 1]),
                    wait=[value[b]] + ([("signed", pr.counts["signed"])] if b else []), done="signed")
    sums = mem.bank(6, B)
    q = pr.add("pe", lambda e: e.matmul(sums, c.ones[:], tally[:], start=True, stop=True), wait=[t0, c.const], done="sign_sum")
    enough = mem.small("enough", B)
    q = pr.add("dve", lambda e: e.tensor_scalar(enough[:], sums, float(TOPK), None, ALU.is_ge), wait=[q], done="signed")
    pr.add("dve", lambda e: e.tensor_scalar(sign[:], enough[:], 2.0, -1.0, ALU.mult, ALU.add), wait=[q], done="signed")
    q = pr.add("dve", lambda e: e.tensor_scalar(rank[:], enough[:], float(2 * TOPK - N - 1), float(N - TOPK + 1), ALU.mult, ALU.add),
               done="signed")
    turned = [None] * B
    for b in range(B):
        turned[b] = pr.add("dve", lambda e, b=b: e.tensor_scalar(flat[b], flat[b], sign[:, b:b + 1], 0.0, ALU.mult, ALU.add),
                           wait=[q], done="signed")

    ON_ACT = 3 * D
    ON_DVE = PER - ON_ACT
    high = mem.small("high", B)
    low = mem.small("low", B)
    goal = mem.small("goal", B)
    bound = mem.small("bound", B)
    base = mem.small("base", B)
    passed = mem.small("passed", B)
    above = mem.small("above", B)

    def to_goal(ready, name):
        pr.add("dve", lambda e: e.tensor_copy(goal[:, 0:B:2], rank[:, 0:B:2]), wait=ready, done=name)
        return pr.add("dve", lambda e: e.tensor_scalar(goal[:, 1:B:2], rank[:, 1:B:2], -0.5 * P * ON_ACT, None, ALU.add), done=name)

    def count(g, data, ready, name):
        a, b = 2 * g, 2 * g + 1
        last_dve = dve_pass.get("at")
        pr.add("dve", lambda e: e.tensor_scalar(junk, data[:, a], bound[:, a:a + 1], 0.0, ALU.is_ge, ALU.add,
                                                accum_out=tally[:, a:a + 1]), wait=ready + [last_dve], done="count_dve")
        mine = ("count_dve", pr.counts["count_dve"])
        t1 = pr.add("dve", lambda e: e.tensor_scalar(junk[:, :ON_DVE], data[:, b, :ON_DVE], bound[:, b:b + 1], 0.0, ALU.is_ge,
                                                     ALU.add, accum_out=tally[:, b:b + 1]), wait=[mine], done="count_dve")
        dve_pass["at"] = t1
        t2 = pr.add("act", lambda e: e.activation(junk_act[:, :ON_ACT], data[:, b, ON_DVE:], ACT.Sign, scale=-1.0,
                                                  bias=bound[:, b:b + 1], accum_out=tally_act[:, b:b + 1]),
                    wait=ready + [dve_pass.get("act")], done="count_act")
        dve_pass["act"] = t2
        s = mem.bank(4 + g, 2)
        pr.add("pe", lambda e: e.matmul(s, c.ones[:], tally[:, a:b + 1], start=True, stop=False, skip_group_check=True),
               wait=[t1, dve_pass.get(("tested", g))])
        return pr.add("pe", lambda e: e.matmul(s[:, 1:2], c.minus_halves, tally_act[:, b:b + 1], start=False, stop=True,
                                               skip_group_check=True), wait=[t2], done=f"counted{g}")

    dve_pass = {}

    def descend(data, bits, ready, name):
        start = pr.add("dve", lambda e: e.memset(bound[:], 2.0 ** (bits - 1) - 0.5), wait=ready, done=name)
        at = [[start] + ready, [start] + ready]
        for bit in reversed(range(bits)):
            value, half = 2.0 ** bit, 2.0 ** (bit - 1)
            counted = [count(g, data, at[g], name) for g in range(2)]
            for g in range(2):
                cols = slice(2 * g, 2 * g + 2)
                b0 = pr.add("dve", lambda e, cols=cols, d=(-value + half if bit else -value): e.tensor_scalar(
                    base[:, cols], bound[:, cols], d, None, ALU.add), wait=at[g], done=name)
                t = pr.add("dve", lambda e, g=g, cols=cols: e.tensor_tensor(passed[:, cols], mem.bank(4 + g, 2), goal[:, cols], ALU.is_ge),
                           wait=[counted[g]], done=name)
                dve_pass["tested", g] = t
                n = pr.add("dve", lambda e, cols=cols, value=value: e.scalar_tensor_tensor(
                    bound[:, cols], passed[:, cols], value, base[:, cols], ALU.mult, ALU.add), wait=[t, b0], done=name)
                at[g] = [n]
        return at[0] + at[1]

    halves = [f.bitcast(INT16).rearrange("p (n two) -> p n two", two=2) for f in flat]
    uhalves = [f.bitcast(UINT16).rearrange("p (n two) -> p n two", two=2) for f in flat]
    for b in range(B):
        eng = "act" if b % 2 else "pool"
        if eng == "act":
            k = pr.add("act", lambda e, b=b: e.activation(keys[:, b], halves[b][:, :, 1], ACT.Copy), wait=[turned[b]], done="keys_act")
        else:
            k2 = pr.add("pool", lambda e, b=b: e.tensor_copy(keys[:, b], halves[b][:, :, 1]), wait=[turned[b]], done="keys_pool")
    gl = to_goal([q], "search")
    hs = descend(keys, 15, [k, k2, gl], "search")
    h = pr.add("dve", lambda e: e.tensor_scalar(high[:], bound[:], 0.5, None, ALU.add), wait=hs, done="search")
    ab = pr.add("dve", lambda e: e.tensor_scalar(base[:], high[:], 0.5, None, ALU.add), wait=[h], done="search")
    for b in range(B):
        a1 = pr.add("dve", lambda e, b=b: e.tensor_scalar(junk, keys[:, b], base[:, b:b + 1], 0.0, ALU.is_ge, ALU.add,
                                                          accum_out=tally[:, b:b + 1]),
                    wait=[ab, dve_pass["at"]] + ([("search", pr.counts["search"])] if b else []), done="search")
    a2 = pr.add("pe", lambda e: e.matmul(sums, c.ones[:], tally[:], start=True, stop=True), wait=[a1], done="above_sum")
    a3 = pr.add("dve", lambda e: e.tensor_tensor(rank[:], rank[:], sums, ALU.subtract), wait=[a2], done="search")
    for b in range(B):
        lw = pr.add("dve", lambda e, b=b: e.scalar_tensor_tensor(lows[:, b], keys[:, b], high[:, b:b + 1], uhalves[b][:, :, 0],
                                                                 ALU.is_equal, ALU.mult), wait=[a1, h], done="lows")
    gl = to_goal([a3], "search")
    ls = descend(lows, 16, [lw, gl], "search")

    pivot = mem.small("pivot", B)
    neg_pivot = mem.small("neg_pivot", B)
    whole = pivot[:].bitcast(INT16).rearrange("p (n two) -> p n two", two=2)
    uwhole = pivot[:].bitcast(UINT16).rearrange("p (n two) -> p n two", two=2)
    l = pr.add("dve", lambda e: e.tensor_scalar(low[:], bound[:], 0.5, None, ALU.add), wait=ls, done="search")
    pr.add("dve", lambda e: e.tensor_copy(whole[:, :, 1], high[:]), wait=[l], done="search")
    pz = pr.add("dve", lambda e: e.tensor_copy(uwhole[:, :, 0], low[:]), done="search")
    eq = mem.view("w_b", 0, FP16, NT, D)
    prefix = mem.view("w_b", 4, FP32, NT, D)
    taken = mem.view("w_b", 12, FP16, NT, D)
    zeros = mem.view("w_b", 16, FP32, D)
    zz = pr.add("pool", lambda e: e.memset(zeros, 0.0), wait=ls, done="zeros")
    n_eq = mem.small("n_eq", B, NT)
    n_gt = mem.small("n_gt", B)
    gt_sign = mem.small("gt_sign", B)
    pv = pr.add("dve", lambda e: e.tensor_tensor(pivot[:], pivot[:], sign[:], ALU.mult), wait=[pz], done="search")
    npv = pr.add("dve", lambda e: e.tensor_scalar(neg_pivot[:], pivot[:], -1.0, None, ALU.mult), wait=[pv], done="search")
    back = [None] * B
    for b in range(B):
        back[b] = pr.add("dve", lambda e, b=b: e.tensor_scalar(flat[b], flat[b], sign[:, b:b + 1], None, ALU.mult), wait=[lw], done="search")
    gt = [pr.add("act", lambda e, b=b: e.activation(junk_act, flat[b], ACT.Sign, bias=neg_pivot[:, b:b + 1],
                                                    accum_out=gt_sign[:, b:b + 1]),
                 wait=[back[b], npv] + ([("gt_sign", pr.counts["gt_sign"])] if b else [dve_pass["act"]]), done="gt_sign") for b in range(B)]
    earlier = mem.small("earlier", B, NT)
    quota = mem.small("quota", B, NT)
    row_eq = mem.small("row_eq", B)
    places = mem.bank(6, B, NT)
    c.x1 = [None] * B
    prev_taken = None
    prev_sel = None
    qdone = None
    zero_earlier = pr.add("dve", lambda e: e.memset(earlier[:, :, 0:1], 0.0), done="quota")
    for b in range(B):
        for t in range(NT):
            ee = pr.add("dve", lambda e, b=b, t=t: e.tensor_scalar(eq[:, t], v[:, b, t], pivot[:, b:b + 1], 0.0, ALU.is_equal, ALU.add,
                                                                   accum_out=n_eq[:, b, t:t + 1]),
                        wait=[back[b], pv, prev_sel] + ls, done="equal")
        for t in range(1, NT):
            er = pr.add("dve", lambda e, b=b, t=t: e.tensor_tensor(earlier[:, b, t:t + 1], earlier[:, b, t - 1:t], n_eq[:, b, t - 1:t], ALU.add),
                        wait=[ee, zero_earlier] + ([er] if t > 1 else []), done="quota")
        er = pr.add("dve", lambda e, b=b: e.tensor_tensor(row_eq[:, b:b + 1], earlier[:, b, NT - 1:NT], n_eq[:, b, NT - 1:NT], ALU.add),
                    wait=[er], done="quota")
        er = pr.add("dve", lambda e, b=b: e.tensor_scalar(n_gt[:, b:b + 1], gt_sign[:, b:b + 1], row_eq[:, b:b + 1], float(PER), ALU.subtract, ALU.add),
                    wait=[er, gt[b]], done="quota")
        er = pr.add("dve", lambda e, b=b: e.scalar_tensor_tensor(earlier[:, b], n_gt[:, b:b + 1].broadcast_to([P, NT]), 0.5, earlier[:, b], ALU.mult, ALU.add),
                    wait=[er], done="quota")
        pr.add("pe", lambda e, b=b: e.matmul(places[:, b], c.before, n_eq[:, b], start=True, stop=False), wait=[ee, a3, qdone])
        pl = pr.add("pe", lambda e, b=b: e.matmul(places[:, b], c.ones[:], earlier[:, b], start=False, stop=True), wait=[er], done="places")
        qu = pr.add("dve", lambda e, b=b: e.tensor_scalar(quota[:, b], places[:, b], -1.0, float(TOPK), ALU.mult, ALU.add), wait=[pl], done="quota")
        qdone = c.places_read = qu
        for t in range(NT):
            sc = pr.add("dve", lambda e, b=b, t=t: e.tensor_tensor_scan(prefix[:, t], eq[:, t], zeros, 0.0, ALU.add, ALU.add),
                        wait=[ee, zz, prev_taken], done="prefix")
            sl = pr.add("dve", lambda e, b=b, t=t: e.scalar_tensor_tensor(taken[:, t], prefix[:, t], quota[:, b, t:t + 1], eq[:, t], ALU.is_le, ALU.mult),
                        wait=[sc, qu, prev_taken], done="taken")
            ga = pr.add("dve", lambda e, b=b, t=t: e.scalar_tensor_tensor(c.x[:, b, t], v[:, b, t], pivot[:, b:b + 1], c.x[:, b, t], ALU.is_gt, ALU.add),
                        done="greater")
            c.x1[b] = pr.add("pool", lambda e, b=b, t=t: e.tensor_tensor(c.x[:, b, t], c.x[:, b, t], taken[:, t], ALU.add), wait=[sl, ga], done="masked")
        prev_taken = c.x1[b]
        prev_sel = sl


def attention(pr, mem, c, w_ih, cond):
    squares = mem.view("cols", 16, FP32, D)
    power = mem.small("row_power", B, NT)
    row_rms = mem.small("row_rms", B, NT)
    for b in range(B):
        for t in range(NT):
            sq = pr.add("act", lambda e, b=b, t=t: e.activation(squares, c.x[:, b, t], ACT.Square, accum_out=power[:, b, t:t + 1]),
                        wait=[c.x1[b]] + ([sq] if b + t else []), done="row_power")
    m = pr.add("dve", lambda e: e.tensor_scalar(row_rms[:], power[:], 1.0 / D, EPS, ALU.mult, ALU.add), wait=[sq], done="inverse_rms")
    m = pr.add("act", lambda e: e.activation(row_rms[:], row_rms[:], ACT.Sqrt), wait=[m], done="row_root")
    rms = pr.add("dve", lambda e: e.reciprocal(row_rms[:], row_rms[:]), wait=[m], done="inverse_rms")

    c.xT = mem.view("cols", 0, FP32, NC, B, S)
    QK = 2 * HEADS
    normed = mem.view("work", 16, FP32, NT, D)
    qk = mem.view("work", 0, FP32, NT, QK, DH)
    sq_qk = mem.view("work", 24, FP32, QK, DH)
    stacks = [mem.view("work", at, FP16, HEADS, 4, DH) for at in (28, 16)]
    probT = mem.view("work", 0, FP32, HPG, NT, S)
    xnT = mem.view("cond", 0, FP32, NC, S)
    qT = mem.view("scratch", 0, FP16, HEADS, S)
    kT = mem.view("w_b", 0, FP16, HEADS, S)
    v = mem.view("w_b", 16, FP32, NT, D)
    oT = mem.view("cond", 0, FP32, NC, S)
    head_power = mem.small("head_power", NT, QK)
    top = mem.small("top", NT * HEADS)
    neg_top = mem.small("neg_top", NT * HEADS)
    weight = mem.small("weight", NT, HEADS)
    last = {}
    bank_read = [c.places_read] * 8
    out_done = None
    for b in range(B):
        probs = mem.view("rows", 8 * b, FP32, 4, S)
        for t in range(NT):
            nr = pr.add("dve", lambda e, b=b, t=t: e.tensor_scalar(normed[:, t], c.x[:, b, t], row_rms[:, b, t:t + 1], None, ALU.mult),
                        wait=[rms, last.get("pv"), c.x1[B - 1]], done="normed")
        for k in range(NC):
            raw, nrm = mem.bank(6, S), mem.bank(7, S)
            for t in range(NT):
                e1 = pr.add("pe", lambda e, b=b, k=k, t=t, raw=raw: e.transpose(raw[:, t * P:(t + 1) * P], c.x[:, b, t, k * P:(k + 1) * P], c.ident[:]),
                            wait=[c.x1[b], bank_read[6], c.w_emb_read], done="x_turned" if t == NT - 1 else None)
            for t in range(NT):
                e2 = pr.add("pe", lambda e, k=k, t=t, nrm=nrm: e.transpose(nrm[:, t * P:(t + 1) * P], normed[:, t, k * P:(k + 1) * P], c.ident[:]),
                            wait=[nr, bank_read[7]], done="normed_turned" if t == NT - 1 else None)
            xc = bank_read[6] = pr.add("dve", lambda e, b=b, k=k, raw=raw: e.tensor_copy(c.xT[:, k, b], raw), wait=[e1, rms, c.w16_done], done="x_cols")
            xn = bank_read[7] = pr.add("act", lambda e, b=b, k=k, nrm=nrm: e.activation(
                xnT[:, k], nrm, ACT.Identity, scale=c.col_scale[:, k, b:b + 1], bias=c.col_shift[:, k, b:b + 1]),
                wait=[e2, c.col_done, out_done, last.get("plus")] + c.cond_read, done="x_normed_cols")
        def project(t):
            banks = [3 * (t % 2) + i for i in range(3)]
            made = [None] * 3
            for i in range(3):
                for k in range(NC):
                    made[i] = pr.add("pe", lambda e, i=i, k=k, t=t, banks=banks: e.matmul(
                        mem.bank(banks[i], D), xnT[:, k, t * P:(t + 1) * P], c.w_qkv[:, k, i * D:(i + 1) * D],
                        start=(k == 0), stop=(k == NC - 1)), wait=[xn, c.w_qkv_in, bank_read[banks[i]]],
                        done="projected" if k == NC - 1 else None)
            last["projected"] = made[2]
            for i in range(2):
                sq = pr.add("act", lambda e, i=i, banks=banks: e.activation(
                    sq_qk[:, i * HEADS:(i + 1) * HEADS], mem.bank(banks[i], HEADS, DH), ACT.Square),
                    wait=[made[i], last.get("sq_read"), last.get("pv"), rms], done="qk_square")
                last["copied"] = bank_read[banks[i]] = pr.add("act", lambda e, i=i, t=t, banks=banks: e.activation(
                    qk[:, t, i * HEADS:(i + 1) * HEADS], mem.bank(banks[i], HEADS, DH), ACT.Copy), done="qk_rows")
            last["sq_read"] = hp = pr.add("dve", lambda e, t=t: e.tensor_reduce(head_power[:, t], sq_qk, AX.X, ALU.add),
                                          wait=[sq, last.get("heads_read")], done="head_power")
            last["values"] = bank_read[banks[2]] = pr.add("dve", lambda e, t=t, banks=banks: e.tensor_copy(v[:, t], mem.bank(banks[2], D)),
                                                          wait=[made[2], last.get("pv")], done="values")
            m = pr.add("dve", lambda e, t=t: e.tensor_scalar(head_power[:, t], head_power[:, t], 1.0 / DH, EPS, ALU.mult, ALU.add),
                       wait=[hp], done="inverse_rms")
            m = pr.add("act", lambda e, t=t: e.activation(head_power[:, t], head_power[:, t], ACT.Sqrt), wait=[m], done="head_root")
            return pr.add("dve", lambda e, t=t: e.reciprocal(head_power[:, t], head_power[:, t]), wait=[m], done="inverse_rms")

        def heads_to_columns(t, m):
            n = pr.add("dve", lambda e, t=t: e.tensor_tensor(qk[:, t], qk[:, t], head_power[:, t].unsqueeze(2).broadcast_to([P, QK, DH]), ALU.mult),
                       wait=[m, last["copied"]], done="qk_normed")
            last["heads_read"] = n
            keyed = pr.add("pool", lambda e, t=t: e.tensor_tensor(
                qk[:, t, HEADS:], qk[:, t, HEADS:], c.gain[:].unsqueeze(1).broadcast_to([P, HEADS, DH]), ALU.mult),
                wait=[n, c.gain_done], done="keys_gained")
            for i in range(2):
                stack = stacks[i]
                src = qk[:, t, i * HEADS:(i + 1) * HEADS].unsqueeze(2).broadcast_to([P, HEADS, 2, DH])
                hi = stack[:, :, 0:2] if i == 0 else stack[:, :, 0:4:2]
                lo = stack[:, :, 2:4] if i == 0 else stack[:, :, 1:4:2]
                s1 = pr.add("act", lambda e, src=src, hi=hi: e.activation(hi, src, ACT.Copy),
                            wait=[n if i == 0 else keyed, last.get(("stack_read", i)), normed_read], done="stack_high")
                for slot in range(2):
                    s2 = pr.add("dve", lambda e, i=i, t=t, hi=hi, lo=lo, slot=slot: e.tensor_tensor(
                        lo[:, :, slot], qk[:, t, i * HEADS:(i + 1) * HEADS], hi[:, :, slot], ALU.subtract),
                        wait=[s1, keyed], done="stack_low")
                for half in range(2):
                    bk = 6 + half
                    to = mem.banks[bk][:].bitcast(FP16).rearrange("p (h n) -> p h n", h=8)
                    for h in range(8):
                        tp = pr.add("pe", lambda e, to=to, h=h, half=half, stack=stack: e.transpose(
                            to[:, h], stack[:, half * 8 + h].rearrange("p a d -> p (a d)"), c.ident16[:]),
                            wait=[s2, bank_read[bk]], done="stack_turned" if h == 7 else None)
                    dst = (qT if i == 0 else kT)[:, half * 8:half * 8 + 8, t * P:(t + 1) * P]
                    w = [tp, last.get("scores"), xc]
                    if half == 0:
                        bank_read[bk] = pr.add("act", lambda e, to=to, dst=dst: e.activation(dst, to, ACT.Copy), wait=w, done="heads_act")
                    else:
                        bank_read[bk] = pr.add("dve", lambda e, to=to, dst=dst: e.tensor_copy(dst, to), wait=w, done="heads_dve")
                last["stack_read", i] = tp

        normed_read = e2
        before = None
        for t in range(NT):
            m = project(t)
            if before is not None:
                heads_to_columns(t - 1, before)
            before = m
        if b == B - 1:
            c.w_ih = mem.view("w_a", 0, FP32, NC, GATES * D)
            c.w_ih_in = pr.dma("sp", c.w_ih, w_ih.rearrange("(k p) n -> p k n", p=P), "w_ih_in", wait=[last["projected"]])
        heads_to_columns(NT - 1, before)
        heads_made = [bank_read[6], bank_read[7]]

        def scores(g, t, pair):
            bks = [2 * pair, 2 * pair + 1]
            col = t * HEADS + g * HPG + 2 * pair
            scored = []
            for i in range(2):
                h = g * HPG + 2 * pair + i
                scored.append(pr.add("pe", lambda e, i=i, h=h, t=t, bks=bks: e.matmul(
                    mem.bank(bks[i], S), qT[:, h, t * P:(t + 1) * P], kT[:, h], start=True, stop=True),
                    wait=heads_made + [bank_read[bks[i]]], done="scores"))
            last["scores"] = scored[1]
            for i in range(2):
                mx = pr.add("dve", lambda e, i=i, bks=bks, col=col: e.tensor_reduce(
                    top[:, col + i:col + i + 1], mem.bank(bks[i], S), AX.X, ALU.max), wait=[scored[i], last.get(("exp", b - 1))], done="top")
            nm = pr.add("dve", lambda e, col=col: e.tensor_scalar(neg_top[:, col:col + 2], top[:, col:col + 2], c.minus_logit_scale[:], None, ALU.mult),
                        wait=[mx, c.gain_done], done="neg_top")
            made = []
            for i in range(2):
                h = g * HPG + 2 * pair + i
                slot = 2 * pair + i
                ex = bank_read[bks[i]] = pr.add("act", lambda e, i=i, h=h, t=t, slot=slot, bks=bks, col=col, probs=probs: e.activation(
                    probs[:, slot], mem.bank(bks[i], S), ACT.Exp, scale=c.logit_scale[:], bias=neg_top[:, col + i:col + i + 1],
                    accum_out=weight[:, t, h:h + 1]), wait=[nm, e1, last.get(("turned", slot)), last.get("weights_read")], done="exp")
                made.append(ex)
            last["exp", b] = last["exp"] = ex
            return made

        def turn(g, t, pair, made):
            for i in range(2):
                slot, bk = 2 * pair + i, 4 + i
                for kt in range(NT):
                    tp = pr.add("pe", lambda e, kt=kt, slot=slot, bk=bk, probs=probs: e.transpose(
                        mem.bank(bk, NT, P)[:, kt], probs[:, slot, kt * P:(kt + 1) * P], c.ident[:]),
                        wait=[made[i], bank_read[bk]], done="probs_turned" if kt == NT - 1 else None)
                last["turned", slot] = tp
                dst = probT[:, 2 * pair + i, :, t * P:(t + 1) * P]
                w = [tp, last.get("pv")]
                if i == 0:
                    bank_read[bk] = pr.add("act", lambda e, bk=bk, dst=dst: e.activation(dst, mem.bank(bk, NT, P), ACT.Copy), wait=w, done="probs_act")
                else:
                    bank_read[bk] = pr.add("dve", lambda e, bk=bk, dst=dst: e.tensor_copy(dst, mem.bank(bk, NT, P)), wait=w, done="probs_dve")

        def weighted_values(g, exp_done):
            for kt in range(NT):
                for i in range(HPG):
                    h = g * HPG + i
                    last["pv"] = pr.add("pe", lambda e, kt=kt, i=i, h=h: e.matmul(
                        mem.banks[6][DH * i:DH * i + DH, :], v[:, kt, h * DH:(h + 1) * DH], probT[:, i, kt],
                        start=(kt == 0), stop=(kt == NT - 1), tile_position=(0, DH * i)),
                        wait=[bank_read[4], bank_read[5], bank_read[6], last["values"]], done="pv" if kt == NT - 1 and i == HPG - 1 else None) or last.get("pv")

        def divide(g, exp_done):
            iv = pr.add("dve", lambda e, g=g: e.reciprocal(
                oT[:, g].rearrange("p (t h d) -> p t h d", t=NT, h=HPG), weight[:, :, g * HPG:(g + 1) * HPG].unsqueeze(3).broadcast_to([P, NT, HPG, DH])),
                        wait=[exp_done, last["projected"], out_done, last.get("plus")], done="inv_weight")
            last["weights_read"] = iv if g == NC - 1 else last.get("weights_read")
            for t in range(NT):
                ic = pr.add("pe", lambda e, g=g, t=t: e.matmul(
                    mem.bank(7, S)[:, t * P:(t + 1) * P], oT[:, g, t * P:(t + 1) * P],
                    c.ident[:], start=True, stop=True), wait=[iv, bank_read[7]], done="inv_turned" if t == NT - 1 else None)
            cpi = bank_read[7] = pr.add("act", lambda e, g=g: e.activation(oT[:, g], mem.bank(7, S), ACT.Copy),
                                        wait=[ic], done="inv_cols")
            last["out_scaled"] = bank_read[6] = pr.add("dve", lambda e, g=g: e.tensor_tensor(oT[:, g], mem.bank(6, S), oT[:, g], ALU.mult),
                                                       wait=[last["pv"], cpi, out_done] + c.cond_read, done="out_cols")

        units = [(g, t, pair) for g in range(NC) for t in range(NT) for pair in range(2)]
        made = scores(*units[0])
        for n_, unit in enumerate(units):
            exp_done = last["exp"]
            following = scores(*units[n_ + 1]) if n_ + 1 < len(units) else None
            turn(*unit, made)
            if unit[1] == NT - 1 and unit[2] == 1:
                weighted_values(unit[0], exp_done)
                divide(unit[0], exp_done)
            made = following
        for m_ in range(NC):
            for k in range(NC):
                wo = pr.add("pe", lambda e, m_=m_, k=k: e.matmul(mem.bank(6 + m_ % 2, S), c.w_out[:, k, m_ * P:(m_ + 1) * P], oT[:, k],
                                                                start=(k == 0), stop=(k == NC - 1)),
                            wait=[last["out_scaled"], c.w_out_in, bank_read[6 + m_ % 2]], done="w_out" if k == NC - 1 else None)
            a1 = pr.add("pool", lambda e, m_=m_, b=b: e.tensor_tensor(c.xT[:, m_, b], c.xT[:, m_, b], oT[:, m_], ALU.add),
                        wait=[last["out_scaled"], xc], done="plus_o")
            a2 = bank_read[6 + m_ % 2] = pr.add("dve", lambda e, m_=m_, b=b: e.tensor_tensor(c.xT[:, m_, b], c.xT[:, m_, b], mem.bank(6 + m_ % 2, S), ALU.add),
                                                wait=[wo, a1], done="plus_w_out")
        out_done = wo
        last["plus"] = a1
    c.x2 = [a2]
    c.attention_over = [a2, wo, a1, last["out_scaled"], last["pv"], last["scores"]]
    c.bank_read = bank_read


def floor_and_weights(pr, mem, c, cond):
    grid = mem.view("cond", 0, FP32, B, D)
    whole = mem.view("w_b", 0, FP32, B, D)
    as_int = mem.view("w_b", 8, INT32, B, D)
    w0 = mem.view("w_b", 8, FP32, B, D)
    right = mem.view("w_b", 16, FP32, B, D)
    c.sampling = mem.view("rows", 0, FP32, B, NC, D)
    part = mem.view("scratch", 12, FP32, 2, D)
    loaded = pr.dma("sp", grid.rearrange("p b d -> p (b d)"), cond.rearrange("b d -> (b d)").partition_broadcast(P),
                    "grid_in", wait=c.attention_over)

    def dve(emit, *wait):
        return pr.add("dve", emit, wait=list(wait), done="grid")

    far = 2.0 ** 24
    g = dve(lambda e: e.tensor_scalar(grid, grid, 1.0, 0.5, ALU.add, ALU.mult), loaded, *c.attention_over)
    g = dve(lambda e: e.tensor_scalar(grid, grid, float(D - 1), far, ALU.mult, ALU.min), g)
    g = dve(lambda e: e.tensor_scalar(grid, grid, -far, None, ALU.max), g)
    g = dve(lambda e: e.tensor_copy(as_int, grid), g)
    g = dve(lambda e: e.tensor_copy(whole, as_int), g)
    g = dve(lambda e: e.tensor_tensor(right, whole, grid, ALU.is_gt), g)
    g = dve(lambda e: e.tensor_tensor(whole, whole, right, ALU.subtract), g)
    w1 = g = dve(lambda e: e.tensor_tensor(grid, grid, whole, ALU.subtract), g)
    dve(lambda e: e.tensor_scalar(w0, grid, -1.0, 1.0, ALU.mult, ALU.add), g)
    g = dve(lambda e: e.tensor_scalar(right, whole, 1.0, 0.0, ALU.add, ALU.max), g)
    dve(lambda e: e.tensor_scalar(right, right, float(D - 1), None, ALU.min), g)
    g = dve(lambda e: e.tensor_scalar(whole, whole, 0.0, float(D - 1), ALU.max, ALU.min), g)
    read = [None, None]
    c.sampling_done = [None] * B
    for b in range(B):
        for k in range(NC):
            to, feature, slot = c.sampling[:, b, k], c.feature[:, k:k + 1], k % 2
            l = dve(lambda e, b=b, to=to, feature=feature: e.scalar_tensor_tensor(
                to, whole[:, b], feature, w0[:, b], ALU.is_equal, ALU.mult), g)
            r = dve(lambda e, b=b, feature=feature, slot=slot: e.scalar_tensor_tensor(
                part[:, slot], right[:, b], feature, grid[:, b], ALU.is_equal, ALU.mult), g, read[slot])
            s = pr.add("pool", lambda e, to=to, slot=slot: e.tensor_tensor(to, to, part[:, slot], ALU.add), wait=[l, r], done="sampling")
            read[slot] = s
            diagonal = to[:, k * P:(k + 1) * P]
            c.sampling_done[b] = pr.add("pool", lambda e, diagonal=diagonal: e.tensor_tensor(diagonal, diagonal, c.ident[:], ALU.add),
                                        wait=[s], done="sampling")
    c.grid_read = c.sampling_done[B - 1]


STEPS_PER_CHUNK = 32
GROUP = 4
UNITS = "AAr AAz ABz AAn BAr BAz BBz BAn ABr BBr ABn BBn".split()
ORDER = ("rsumA zsumA zaddA rsigA zsumB zsigA nmulA nsumA tanhA rsumB omzA zaddB zhA rsigB tmulA zsplitA nmulB "
         "zlowA tlowA zsigB zhB nsumB omzB zsplitB tanhB nputA stateA tmulB zlowB stateB rputB tlowB rputA nputB").split()


def gru(pr, mem, c, cond, out):
    state = mem.view("work", 0, FP32, S + 1, NC, B)
    gates_in = mem.view("scratch", 0, FP32, 2, 2 * GATES * 2, B, STEPS_PER_CHUNK)
    bias_in = mem.small("bias_in", 2, GATES, 2)
    n_bias = mem.small("n_bias", 2, 2)
    parts = [[mem.small(f"parts{parity}{half}", 2, 4, B, dtype=FP16) for half in "AB"] for parity in range(2)]
    rz = [mem.small(f"rz{h}", 4, B) for h in "AB"]
    gate = [mem.small(f"gate{h}", 4, B) for h in "AB"]
    nm = [mem.small(f"nm{h}", 2, 6, B) for h in "AB"]
    nsum = [mem.small(f"nsum{h}", 2, B) for h in "AB"]
    new = [mem.small(f"new{h}", 2, B) for h in "AB"]
    one_minus_z = [mem.small(f"one_minus_z{h}", 2, B) for h in "AB"]
    t_ = [mem.small(f"t{h}", 2, B) for h in "AB"]
    zh = [mem.small(f"zh{h}", 2, B) for h in "AB"]
    rows_out = mem.view("w_b", 0, FP32, 4, D)
    r_bank, z_bank, n_bank, side_bank = (0, 1), (2, 3), (4, 5), (6, 7)

    def of_bank(bank):
        return mem.bank(bank, 2, 5, B)

    over = c.attention_over
    both = mem.small("both", GATES, NC)
    for half in range(2):
        cleared = pr.add("pool", lambda e, half=half: e.memset(parts[0][half][:], 0.0), done="gru_ready")
    pr.add("dve", lambda e: e.tensor_copy(both[:], c.b_ih[:]), wait=[c.small_in, c.scale], done="gru_first")
    bi = ("gru_first", pr.counts["gru_first"])
    bi = pr.add("dve", lambda e: e.tensor_tensor(both[:, :2], c.b_ih[:, :2], c.b_hh[:, :2], ALU.add), wait=[bi], done="gru_first")
    bi = pr.add("dve", lambda e: e.tensor_scalar(bias_in[:].rearrange("p m g c -> p g m c"), both[:].rearrange("p g (m c) -> p g m c", c=2),
                                                 c.gate_scale[:], None, ALU.mult), wait=[bi], done="gru_first")
    for half in range(2):
        pr.add("dve", lambda e, half=half: e.tensor_scalar(
            of_bank(n_bank[half])[:, :, 4], c.b_hh[:, 2, 2 * half:2 * half + 2].unsqueeze(2).broadcast_to([P, 2, B]), c.gate_scale[:], None, ALU.mult),
            wait=[c.bank_read[n_bank[half]]] + over, done="gru_first")
    first = pr.add("dve", lambda e: e.tensor_scalar(state[:, 0], c.condT[:].rearrange("p b k -> p k b"), c.h_scale[:], None, ALU.mult),
                   wait=over, done="gru_first")
    c.first_state = first
    for half in range(2):
        chunks = slice(2 * half, 2 * half + 2)
        hi = pr.add("dve", lambda e, half=half, chunks=chunks: e.tensor_copy(parts[0][half][:, :, 2], state[:, 0, chunks]),
                    wait=[first, cleared], done="gru_first")
        ready = pr.add("dve", lambda e, half=half, chunks=chunks: e.tensor_tensor(
            parts[0][half][:, :, 3], state[:, 0, chunks], parts[0][half][:, :, 2], ALU.subtract), wait=[hi], done="gru_first")

    registers = {}

    def load_scales(e):
        for name, source in (("unscale", c.gate_unscale), ("scale", c.gate_scale)):
            registers[name] = e.alloc_register(f"act_{name}")
            e.reg_load(registers[name], source[0:1, 0:1].bitcast(INT32))
    pr.add("act", load_scales, wait=[c.scale])

    side_read = {6: c.bank_read[6], 7: c.bank_read[7]}
    side_count = [0]
    gates_made = {}
    gates_free = {}

    def side_matmul(bank, lhs, rhs, k, wait, done=None):
        return pr.add("pe", lambda e: e.matmul(mem.bank(bank, P), lhs, rhs, start=(k == 0), stop=(k == GROUP - 1)),
                      wait=wait + [side_read[bank]], done=done)

    def gate_group(q, j):
        bank = side_bank[side_count[0] % 2]
        side_count[0] += 1
        m, g, ch = j // 6, j % 6 // 2, j % 2
        block = g * NC + 2 * m + ch
        for k in range(NC):
            made = side_matmul(bank, c.w_ih[:, k, block * P:(block + 1) * P], c.xT[:, k, :, q * STEPS_PER_CHUNK:(q + 1) * STEPS_PER_CHUNK],
                               k, [c.w_ih_in] + c.x2, "gates_in_sum" if k == NC - 1 else None)
            if k < NC - 1:
                yield None
        def take():
            side_read[bank] = gates_made[q] = pr.add("act", lambda e: e.activation(
                gates_in[:, q % 2, j], mem.bank(bank, B, STEPS_PER_CHUNK), ACT.Identity, scale=registers["scale"],
                bias=bias_in[:, m, g, ch:ch + 1]), wait=[made, bi] + gates_free.get(q, []), done="gates_in")
        yield take

    rows_read = [None] * 4
    rows_count = [0]
    x3_made = {}

    def rows_group(tile, b, quarter):
        bank = side_bank[side_count[0] % 2]
        side_count[0] += 1
        slot = rows_count[0] // 4 % 4
        rows_count[0] += 1
        cols = slice(quarter * P, (quarter + 1) * P)
        for k in range(NC):
            made = side_matmul(bank, c.xT[:, k, b, tile * P:(tile + 1) * P], c.sampling[:, b, k, cols], k,
                               [x3_made[tile, b], c.sampling_done[b]], "rows_sum" if k == NC - 1 else None)
            if k < NC - 1:
                yield None
        def take():
            side_read[bank] = taken = pr.add("act", lambda e: e.activation(rows_out[:, slot, cols], mem.bank(bank, P), ACT.Copy),
                                             wait=[made, rows_read[slot], c.grid_read], done="rows_out")
            if quarter == 3:
                rows_read[slot] = c.out_event = pr.dma("sp", out[b, tile * P:(tile + 1) * P], rows_out[:, slot], f"out{slot}", wait=[taken])
        yield take

    for j in range(12):
        for item in gate_group(0, j):
            if item:
                item()

    def add_states(tile, b, k, ready):
        x3_made[tile, b] = pr.add("dve", lambda e: e.scalar_tensor_tensor(
            c.xT[:, k, b, tile * P:(tile + 1) * P], state[:, 1 + tile * P:1 + (tile + 1) * P, k, b], c.h_unscale[:],
            c.xT[:, k, b, tile * P:(tile + 1) * P], ALU.mult, ALU.add), wait=ready, done="x3")

    rs_read, zs_read, nm_read, nsum_read = [c.bank_read[i] for i in (0, 1)], [c.bank_read[i] for i in (2, 3)], \
        [c.bank_read[i] for i in (4, 5)], [None, None]
    parts_ready = [[ready], [ready]]
    at = {u: i for i, u in enumerate(UNITS)}
    last_unit = {(h, g): max((k + "AB"[h] + g for k in "AB"), key=at.get) for h in range(2) for g in "rzn"}
    side, groups = None, []
    add_queue = []
    h_last = None
    put = {}
    z_put = any(x.startswith("zput") for x in ORDER)

    def put_gate(s, half, g):
        if s == S:
            return
        q, ss = s // STEPS_PER_CHUNK, s % STEPS_PER_CHUNK
        source = gates_in[:, q % 2, 6 * half + 2 * g:6 * half + 2 * g + 2, :, ss]
        if g == 2:
            put[half, g] = pr.add("pool", lambda e: e.tensor_copy(nm[half][:, :, 5], source),
                                  wait=[gates_made[q], nsum_read[half]], done=f"n_in{half}")
        else:
            put[half, g] = pr.add("act", lambda e: e.activation(of_bank((r_bank, z_bank)[g][half])[:, :, 4], source, ACT.Copy),
                                  wait=[gates_made[q], (rs_read, zs_read)[g][half]], done=f"{'rz'[g]}_in{half}")

    for half in range(2):
        for g in ((0, 1, 2) if z_put else (0, 2)):
            put_gate(0, half, g)
    ev = {}
    for s in range(S):
        q, ss, now, nxt = s // STEPS_PER_CHUNK, s % STEPS_PER_CHUNK, s % 2, (s + 1) % 2
        gi = gates_in[:, q % 2, :, :, ss]
        summed, started = {}, set()
        for u in UNITS:
            read, half, g = "AB".index(u[0]), "AB".index(u[1]), "rzn".index(u[2])
            bank = (r_bank, z_bank, n_bank)[g][half]
            for ch in range(2):
                for k in range(2):
                    for part in range(2):
                        start = (half, g) not in started
                        started.add((half, g))
                        final = last_unit[half, u[2]] == u and ch == k == part == 1
                        product = pr.add("pe", lambda e, bank=bank, ch=ch, part=part, k=k, read=read, j=6 * half + 2 * g + ch, now=now, start=start: e.matmul(
                            mem.bank(bank, 2, 5 * B)[:, ch, :4 * B], c.w16[:, part, 2 * read + k, j], parts[now][read][:, k].rearrange("p q b -> p (q b)"),
                            start=start, stop=(read == 1), skip_group_check=True),
                            wait=parts_ready[read] + ([(rs_read, zs_read, nm_read)[g][half], put.get((half, g))] if start and g < 2 else [nm_read[half]] if start else []) + [c.w16_done], done=f"{u[2]}_products{u[1]}" if final else None)
                        if final:
                            summed[half, u[2]] = product
        if ss == 0:
            assert side is None and not groups
            if q + 1 < S // STEPS_PER_CHUNK:
                gate_groups = [lambda j=j, q=q: gate_group(q + 1, j) for j in range(12)]
            else:
                gate_groups = []
            rows_groups = []
            for i in range(4):
                index = (s - P) // 8 + i
                if index >= 0:
                    rows_groups.append(lambda index=index: rows_group(index // 16, index % 16 // 4, index % 4))
            for i in range(4):
                groups += gate_groups[3 * i:3 * i + 3] + rows_groups[i:i + 1]
            gates_free[q + 1] = list(put.values()) + [ev.get(("zadd", h)) for h in range(2)] if s else []
        takes = []
        if side is None and groups:
            side = groups.pop(0)()
        if side is not None:
            for _ in range(2):
                item = next(side, None)
                if item is not None:
                    takes.append(item)
                    side = None
                    break

        ev = {}
        h_before = [c.first_state, c.first_state] if s == 0 else h_before
        for name in ORDER:
            op, half = name[:-1], "AB".index(name[-1])
            chunks = slice(2 * half, 2 * half + 2)
            key = lambda n: ev[n, half]

            def add(engine, emit, *wait, op=op, half=half):
                ev[op, half] = pr.add(engine, emit, wait=list(wait), done=f"{op}{half}")
                return ev[op, half]

            if op == "rsum":
                rs_read[half] = add("dve", lambda e, half=half: e.tensor_reduce(
                    rz[half][:, 0:2], of_bank(r_bank[half]).rearrange("p c q b -> p c b q"), AX.X, ALU.add), summed[half, "r"], put[half, 0])
            elif op == "zsum":
                zs_read[half] = add("dve", lambda e, half=half: e.tensor_reduce(
                    rz[half][:, 2:4], of_bank(z_bank[half])[:, :, :5 if z_put else 4].rearrange("p c q b -> p c b q"), AX.X, ALU.add),
                    summed[half, "z"], put.get((half, 1)))
            elif op == "zadd":
                add("dve", lambda e, half=half, gi=gi: e.tensor_tensor(rz[half][:, 2:4], rz[half][:, 2:4], gi[:, 6 * half + 2:6 * half + 4], ALU.add),
                    key("zsum"))
            elif op == "rsig":
                add("act", lambda e, half=half: e.activation(gate[half][:, 0:2], rz[half][:, 0:2], ACT.Sigmoid, scale=registers["unscale"]),
                    key("rsum"))
            elif op == "zsig":
                add("act", lambda e, half=half: e.activation(gate[half][:, 2:4], rz[half][:, 2:4], ACT.Sigmoid, scale=registers["unscale"]),
                    key("zsum" if z_put else "zadd"))
            elif op == "nmul":
                nm_read[half] = add("dve", lambda e, half=half: e.tensor_tensor(
                    nm[half][:, :, 0:5], of_bank(n_bank[half]), gate[half][:, 0:2].unsqueeze(2).broadcast_to([P, 2, 5, B]), ALU.mult),
                    summed[half, "n"], key("rsig"))
            elif op == "nsum":
                nsum_read[half] = add("dve", lambda e, half=half: e.tensor_reduce(
                    nsum[half][:], nm[half][:].rearrange("p c q b -> p c b q"), AX.X, ALU.add), key("nmul"), put[half, 2])
            elif op == "tanh":
                add("act", lambda e, half=half: e.activation(new[half][:], nsum[half][:], ACT.Tanh, scale=registers["unscale"]), key("nsum"))
            elif op == "omz":
                add("dve", lambda e, half=half: e.tensor_scalar(one_minus_z[half][:], gate[half][:, 2:4], 1.0, c.minus_h_scale[:],
                                                               ALU.subtract, ALU.mult), key("zsig"))
            elif op == "zh":
                add("dve", lambda e, half=half, chunks=chunks, s=s: e.tensor_tensor(zh[half][:], gate[half][:, 2:4], state[:, s, chunks], ALU.mult),
                    key("zsig"), h_before[half])
            elif op == "zsplit":
                add("act", lambda e, half=half, nxt=nxt: e.activation(parts[nxt][half][:, :, 2], zh[half][:], ACT.Copy), key("zh"))
            elif op == "zlow":
                add("pool", lambda e, half=half, nxt=nxt: e.tensor_tensor(parts[nxt][half][:, :, 3], zh[half][:], parts[nxt][half][:, :, 2],
                                                                         ALU.subtract), key("zsplit"), key("zh"))
            elif op == "tmul":
                t_f = add("dve", lambda e, half=half: e.tensor_tensor(t_[half][:], new[half][:], one_minus_z[half][:], ALU.mult),
                          key("tanh"), key("omz"), h_before[half])
                ev["t16", half] = pr.add("dve", lambda e, half=half, nxt=nxt: e.tensor_tensor(
                    parts[nxt][half][:, :, 0], new[half][:], one_minus_z[half][:], ALU.mult), done=f"t16{half}")
            elif op == "tlow":
                add("dve", lambda e, half=half, nxt=nxt: e.tensor_tensor(parts[nxt][half][:, :, 1], t_[half][:], parts[nxt][half][:, :, 0],
                                                                        ALU.subtract), key("tmul"), key("t16"))
            elif op in ("rput", "zput", "nput"):
                put_gate(s + 1, half, "rzn".index(op[0]))
            elif op == "state":
                ev["state", half] = pr.add("pool", lambda e, half=half, chunks=chunks, s=s: e.tensor_tensor(
                    state[:, s + 1, chunks], t_[half][:], zh[half][:], ALU.add), wait=[key("tmul"), key("zh")], done="state")
        parts_ready = [[ev["zlow", h], ev["tlow", h], ev["zsplit", h]] for h in range(2)]
        h_before = [ev["state", h] for h in range(2)]
        for take in takes:
            take()
        if (s + 1) % P == 0:
            add_queue += [(s // P, b, k) for b in range(B) for k in range(NC)]
        if add_queue and s + 1 < S:
            add_states(*add_queue.pop(0), [ev["state", 1]])
        c.state_done = ev["state", 1]
    return dict(state=state, add_states=add_states, add_queue=add_queue, x3_made=x3_made, rows_out=rows_out, rows_read=rows_read)


def last_tile(pr, mem, c, left, out):
    tile = NT - 1
    while left["add_queue"]:
        left["add_states"](*left["add_queue"].pop(0), [c.state_done])
    events = []
    for b in range(B):
        for k in range(NC):
            made = pr.add("pe", lambda e, b=b, k=k: e.matmul(mem.bank(b, D), c.xT[:, k, b, tile * P:(tile + 1) * P], c.sampling[:, b, k],
                                                            start=(k == 0), stop=(k == NC - 1)),
                          wait=[left["x3_made"][tile, b], c.sampling_done[b]], done="last_rows" if k == NC - 1 else None)
        slot = b
        engine = ("act", "dve")[b % 2]
        emit = (lambda e, b=b, slot=slot: e.activation(left["rows_out"][:, slot], mem.bank(b, D), ACT.Copy)) if engine == "act" else \
            (lambda e, b=b, slot=slot: e.tensor_copy(left["rows_out"][:, slot], mem.bank(b, D)))
        taken = pr.add(engine, emit, wait=[made, left["rows_read"][slot]], done=f"last_taken_{engine}")
        events.append(pr.dma("sp", out[b, tile * P:(tile + 1) * P], left["rows_out"][:, slot], f"out{slot}", wait=[taken]))
    pr.add("sp", None, wait=events)


_INS = ["x", "fside_BxSx1_0", "cond_2048", "L1_cond_W_emb", "L1_cond_b_emb", "L1_cond_g_norm", "L1_cond_W_qkv", "L1_cond_g_q",
        "L1_cond_g_k", "L1_cond_W_out", "L2_cond_W_ih", "L2_cond_W_hh", "L2_cond_b_ih", "L2_cond_b_hh"]


def kernel(**inputs):
    import numpy as _np
    import concourse.bacc as _bacc
    from concourse import mybir as _mybir
    from concourse.bass_utils import run_bass_kernel_spmd as _run

    nc = _bacc.Bacc("TRN2", target_bir_lowering=False, num_devices=1)
    arrays, args = {}, []
    for name in _INS:
        a = _np.ascontiguousarray(inputs[name])
        arrays[f"in_{name}_dram"] = a
        args.append(nc.dram_tensor(f"in_{name}_dram", a.shape, _mybir.dt.from_np(a.dtype), kind="ExternalInput").ap())
    out = nc.dram_tensor("out_dram", (B, S, D), FP32, kind="ExternalOutput").ap()
    build(nc, *args, out)
    r = _run(nc, [arrays], core_ids=[0])
    return r.results[0]["out_dram"]
```

```python
from contextlib import ExitStack

import concourse.bass as bass
from concourse import mybir
from concourse.alu_op_type import AluOpType as ALU

FP32 = mybir.dt.float32
FP16 = mybir.dt.float16
INT32 = mybir.dt.int32
INT16 = mybir.dt.int16
UINT16 = mybir.dt.uint16
ACT = mybir.ActivationFunctionType
AX = mybir.AxisListType

P = 128
B, S, D = 4, 512, 512
NT = S // P
NC = D // P
TOPK = 5120
HEADS = 16
DH = D // HEADS
HPG = P // DH
GATES = 3
EPS = 1e-6
LOWEST = -3.0e38


class Program:

    ENGINES = {"pe": "tensor", "dve": "vector", "act": "scalar", "pool": "gpsimd", "sp": "sync"}

    def __init__(self, nc, ctx):
        self.nc, self.ctx = nc, ctx
        self.queues = {e: [] for e in self.ENGINES}
        self.semaphores, self.counts, self.waited = {}, {}, {}

    def add(self, engine, emit, wait=(), done=None, by=1):
        waits = []
        for event in wait:
            if event is not None and self.waited.get((engine, event[0]), 0) < event[1]:
                self.waited[engine, event[0]] = event[1]
                waits.append(event)
        if done is not None:
            if done not in self.semaphores:
                self.semaphores[done] = self.ctx.enter_context(self.nc.semaphore(done))
                self.counts[done] = 0
            self.counts[done] += by
        made = None if done is None else (done, self.counts[done])

        def run(eng):
            for name, value in waits:
                eng.wait_ge(self.semaphores[name], value)
            instruction = emit(eng) if emit is not None else None
            if made is not None:
                instruction.then_inc(self.semaphores[done], by)

        self.queues[engine].append(run)
        return made

    def dma(self, engine, out, in_, done, wait=(), by_element=False):
        return self.add(engine, lambda e: e.dma_start(out, in_, allow_slow_non_contiguous=by_element), wait, done, 16)

    def emit(self):
        with self.nc.Block() as block:
            for name, attribute in self.ENGINES.items():
                def run(eng, name=name):
                    for item in self.queues[name]:
                        item(eng)
                {"tensor": block.tensor, "vector": block.vector, "scalar": block.scalar,
                 "gpsimd": block.gpsimd, "sync": block.sync}[attribute](run)


class Memory:

    def __init__(self, nc, ctx):
        self.nc, self.ctx = nc, ctx
        self.banks = [ctx.enter_context(nc.psum_tensor(f"bank{i}", [P, 512], FP32)) for i in range(8)]
        kib = {"rows": 32, "cols": 32, "work": 32.25, "cond": 8, "w_a": 24, "w_out": 8, "w_b": 24,
               "w_hh": 24, "scratch": 16}
        self.regions = {n: ctx.enter_context(nc.sbuf_tensor(f"region_{n}", [P, int(k * 256)], FP32))
                        for n, k in kib.items()}

    def view(self, region, at_kib, dtype, *shape):
        n = 1
        for s in shape:
            n *= s
        words = n * {FP32: 4, INT32: 4, FP16: 2, INT16: 2, UINT16: 2}[dtype] // 4
        flat = self.regions[region][:, int(at_kib * 256):int(at_kib * 256) + words]
        if dtype is not FP32:
            flat = flat.bitcast(dtype)
        names = " ".join(f"d{i}" for i in range(len(shape)))
        sizes = {f"d{i}": s for i, s in enumerate(shape[1:], 1)}
        return flat.rearrange(f"p ({names}) -> p {names}", **sizes) if len(shape) > 1 else flat

    def small(self, name, *shape, dtype=FP32):
        return self.ctx.enter_context(self.nc.sbuf_tensor(name, [P, *shape], dtype))

    def bank(self, i, *shape, at=0):
        n = 1
        for s in shape:
            n *= s
        names = " ".join(f"d{j}" for j in range(len(shape)))
        sizes = {f"d{j}": s for j, s in enumerate(shape[1:], 1)}
        flat = self.banks[i][:, at:at + n]
        return flat.rearrange(f"p ({names}) -> p {names}", **sizes) if len(shape) > 1 else flat


def build(nc, x, fside, cond, w_emb, b_emb, g_norm, w_qkv, g_q, g_k, w_out, w_ih, w_hh, b_ih, b_hh, out,
          debug=None):
    with ExitStack() as ctx:
        pr = Program(nc, ctx)
        mem = Memory(nc, ctx)
        c = constants(pr, mem)
        load(pr, mem, c, x, fside, cond, w_emb, b_emb, g_norm, w_qkv, g_q, g_k, w_out, w_ih, w_hh, b_ih, b_hh)
        top_k(pr, mem, c, during_search=lambda: scales(pr, mem, c))
        if debug == "mask":
            for b in range(B):
                dump(pr, out, c.x[:, b], b, c)
            pr.emit()
            return
        attention(pr, mem, c, w_ih, cond)
        if debug == "attn":
            dump_cols(pr, out, c.xT, c)
            pr.emit()
            return
        jobs = floor_and_weights(pr, mem, c, cond)
        left = gru(pr, mem, c, jobs, out)
        last_tile(pr, mem, c, left, out)
        pr.emit()


def dump(pr, out, src, b, c):
    e = pr.dma("sp", out[b].rearrange("(t p) d -> p t d", p=P), src, f"dump{b}", wait=[c.x1[b]])
    pr.add("sp", None, wait=[e])


def dump_cols(pr, out, xT, c):
    for b in range(B):
        e = pr.dma("sp", out[b].rearrange("(p k) s -> p k s", k=NC), xT[:, :, b, :], f"dumpc", wait=c.x2)
    pr.add("sp", None, wait=[e])


class Names:
    pass


def constants(pr, mem):
    c = Names()
    c.ident = mem.small("ident", P)
    c.ident16 = mem.small("ident16", P, dtype=FP16)
    c.ones = mem.small("ones", P)
    c.minus_halves = mem.view("cols", 25, FP32, P)
    c.before = mem.view("cols", 25.5, FP32, P)
    c.feature = mem.small("feature", NC)
    pr.add("pool", lambda e: e.memset(c.ident[:], 0.0), done="const0")
    pr.add("pool", lambda e: e.memset(c.ident16[:], 0.0), done="const0")
    pr.add("pool", lambda e: e.memset(c.ones[:], 1.0), done="const0")
    z = pr.add("pool", lambda e: e.memset(c.minus_halves, -0.5), done="const0")
    for m in (c.ident, c.ident16):
        pr.add("pool", lambda e, m=m: e.affine_select(out=m[:], in_=m[:], compare_op=ALU.not_equal, fill=1.0,
                                                     base=0, pattern=[[-1, P]], channel_multiplier=1),
               wait=[z], done="const")
    pr.add("pool", lambda e: e.affine_select(out=c.before, in_=c.ones[:], compare_op=ALU.is_gt, fill=0.0,
                                             base=0, pattern=[[1, P]], channel_multiplier=-1), wait=[z], done="const")
    c.const = pr.add("pool", lambda e: e.iota(c.feature[:], [[P, NC]], base=0, channel_multiplier=1,
                                              allow_small_or_imprecise_dtypes=True), done="const")
    return c


def load(pr, mem, c, x, fside, cond, w_emb, b_emb, g_norm, w_qkv, g_q, g_k, w_out, w_ih, w_hh, b_ih, b_hh):
    c.x = mem.view("rows", 0, FP32, B, NT, D)
    c.cond_rows = mem.view("cond", 0, FP32, B, D)
    c.fside = mem.small("fside", B, NT)
    c.condT = mem.small("condT", B, NC)
    c.b_emb = mem.small("b_emb", 2 * NC)
    c.g_norm = mem.small("g_norm", NC)
    c.g_q = mem.small("g_q", DH)
    c.g_k = mem.small("g_k", DH)
    c.b_ih = mem.small("b_ih", GATES, NC)
    c.b_hh = mem.small("b_hh", GATES, NC)
    c.w_hh_raw = [mem.view(region, at, FP32, GATES * D) for region, at in
                  (("scratch", 0), ("scratch", 6), ("cols", 26), ("w_b", 18))]
    c.w_emb = mem.view("cols", 0, FP32, NC, 2 * D)
    c.w_qkv = mem.view("w_a", 0, FP32, NC, GATES * D)
    c.w_out = mem.view("w_out", 0, FP32, NC, D)
    c.x_in = [None] * B
    c.x_in[0] = pr.dma("sp", c.x[:, 0], x[0].rearrange("(t p) d -> p t d", p=P), "x_in0")
    c.cond_in = pr.dma("act", c.cond_rows.rearrange("p b d -> p (b d)"),
                       cond.rearrange("b d -> (b d)").partition_broadcast(P), "cond_in")
    for b in range(B):
        c.fside_in = pr.dma("act", c.fside[:, b], fside[b].rearrange("(t p) o -> p (t o)", p=P), "fside_in", by_element=True)
    for b in range(1, B):
        c.x_in[b] = pr.dma("sp", c.x[:, b], x[b].rearrange("(t p) d -> p t d", p=P), f"x_in{b}")
    for b in range(B):
        pr.dma("sp", c.condT[:, b], cond[b].rearrange("(k p) -> p k", p=P), "small_in", by_element=True)
    pr.dma("sp", c.b_emb[:], b_emb.rearrange("(k p) -> p k", p=P), "small_in", by_element=True)
    pr.dma("sp", c.g_norm[:], g_norm.rearrange("(k p) -> p k", p=P), "small_in", by_element=True)
    pr.dma("sp", c.g_q[:], g_q.partition_broadcast(P), "small_in")
    pr.dma("sp", c.g_k[:], g_k.partition_broadcast(P), "small_in")
    pr.dma("sp", c.b_ih[:], b_ih.rearrange("(g k p) -> p g k", p=P, k=NC), "small_in", by_element=True)
    c.small_in = pr.dma("sp", c.b_hh[:], b_hh.rearrange("(g k p) -> p g k", p=P, k=NC), "small_in", by_element=True)
    for k in range(NC):
        c.w_hh_in = pr.dma("sp", c.w_hh_raw[k], w_hh[k * P:(k + 1) * P], "w_hh_in")
    c.w_emb_in = pr.dma("sp", c.w_emb, w_emb.rearrange("(k p) n -> p k n", p=P), "w_emb_in")
    c.w_qkv_in = pr.dma("sp", c.w_qkv, w_qkv.rearrange("(k p) n -> p k n", p=P), "w_qkv_in")
    c.w_out_in = pr.dma("sp", c.w_out, w_out.rearrange("(k p) n -> p k n", p=P), "w_out_in")


def power_of_two(pr, name, dst, src, wait):
    return pr.add("dve", lambda e: e.tensor_scalar(dst.bitcast(INT32), src.bitcast(INT32), 0x7F800000, None,
                                                   ALU.bitwise_and), wait=wait, done=name)


def scales(pr, mem, c):
    chunk_most = mem.small("chunk_most", NC)
    most = mem.small("most", 3)
    absmax = mem.small("absmax", 3)
    c.gain = mem.small("gain", DH)
    gains = pr.add("dve", lambda e: e.tensor_tensor(c.gain[:], c.g_q[:], c.g_k[:], ALU.mult),
                   wait=[c.small_in], done="prepared")
    pr.add("dve", lambda e: e.tensor_reduce(most[:, 2:3], c.gain[:], AX.X, ALU.max, apply_absolute_value=True),
           wait=[gains], done="prepared")
    pr.add("dve", lambda e: e.tensor_reduce(most[:, 1:2], c.condT[:].rearrange("p b k -> p (b k)"), AX.X, ALU.max,
                                            apply_absolute_value=True), done="prepared")
    for k in range(NC):
        m = pr.add("dve", lambda e, k=k: e.tensor_reduce(chunk_most[:, k:k + 1], c.w_hh_raw[k], AX.X, ALU.max,
                                                         apply_absolute_value=True), wait=[c.w_hh_in], done="prepared")
    m = pr.add("dve", lambda e: e.tensor_reduce(most[:, 0:1], chunk_most[:], AX.X, ALU.max), wait=[m], done="prepared")
    r = pr.add("pool", lambda e: e.partition_all_reduce(absmax[:], most[:], P, bass.bass_isa.ReduceOp.max),
               wait=[m], done="absmax")
    guarded = mem.small("guarded", 3)
    pr.add("dve", lambda e: e.tensor_scalar(guarded[:, 0:3:2], absmax[:, 0:3:2], 2.0 ** -60, None, ALU.max),
           wait=[r], done="prepared")
    g = pr.add("dve", lambda e: e.tensor_scalar(guarded[:, 1:2], absmax[:, 1:2], 1.0, None, ALU.max), done="prepared")
    power = mem.small("power", 3)
    p = power_of_two(pr, "prepared", power[:], guarded[:], [g])
    inverse = mem.small("inverse", 3)
    i = pr.add("dve", lambda e: e.reciprocal(inverse[:], power[:]), wait=[p], done="prepared")
    c.w_scale = mem.small("w_scale", 1)
    c.h_scale = mem.small("h_scale", 1)
    c.h_unscale = mem.small("h_unscale", 1)
    c.gate_scale = mem.small("gate_scale", 1)
    c.gate_unscale = mem.small("gate_unscale", 1)
    c.minus_h_scale = mem.small("minus_h_scale", 1)
    pr.add("dve", lambda e: e.tensor_scalar(c.w_scale[:], inverse[:, 0:1], 2.0 ** 13, None, ALU.mult), wait=[i], done="prepared")
    pr.add("dve", lambda e: e.tensor_scalar(c.minus_h_scale[:], inverse[:, 1:2], -2.0 ** 12, None, ALU.mult), done="prepared")
    pr.add("dve", lambda e: e.tensor_scalar(c.h_unscale[:], power[:, 1:2], 2.0 ** -12, None, ALU.mult), done="prepared")
    s0 = pr.add("dve", lambda e: e.tensor_scalar(c.h_scale[:], inverse[:, 1:2], 2.0 ** 12, None, ALU.mult), done="prepared")
    pr.add("dve", lambda e: e.tensor_scalar(c.gate_scale[:], c.w_scale[:], c.h_scale[:], None, ALU.mult), wait=[s0], done="prepared")
    s1 = pr.add("dve", lambda e: e.tensor_scalar(c.gate_unscale[:], power[:, 0:1], 2.0 ** -13, None, ALU.mult), done="prepared")
    c.scale = pr.add("dve", lambda e: e.tensor_scalar(c.gate_unscale[:], c.gate_unscale[:], c.h_unscale[:], None, ALU.mult),
                     wait=[s1], done="prepared")
    c.logit_scale = mem.small("logit_scale", 1)
    c.minus_logit_scale = mem.small("minus_logit_scale", 1)
    pr.add("dve", lambda e: e.tensor_scalar(c.gain[:], c.gain[:], inverse[:, 2:3], None, ALU.mult), wait=[i, gains], done="prepared")
    pr.add("dve", lambda e: e.tensor_scalar(c.minus_logit_scale[:], power[:, 2:3], -float(DH) ** -0.5, None, ALU.mult), done="prepared")
    c.gain_done = pr.add("dve", lambda e: e.tensor_scalar(c.logit_scale[:], power[:, 2:3], float(DH) ** -0.5, None, ALU.mult),
                         done="prepared")

    c.w16 = mem.view("w_hh", 0, FP16, 2, NC, 2 * GATES * 2, P)
    for k in range(NC):
        raw = c.w_hh_raw[k]
        scaled = pr.add("pool", lambda e, raw=raw: e.tensor_tensor(raw, raw, c.w_scale[:].broadcast_to([P, GATES * D]), ALU.mult),
                        wait=[c.scale], done="w_scaled")
        for g in range(GATES):
            src = raw[:, g * D:(g + 1) * D].rearrange("p (m c n) -> p m c n", m=2, c=2)
            parts = [c.w16[:, part, k].rearrange("p (m g c) n -> p m g c n", m=2, g=GATES)[:, :, g] for part in range(2)]
            hi = pr.add("pool", lambda e, src=src, parts=parts: e.tensor_copy(parts[0], src), wait=[scaled], done="w_high")
            c.w16_done = pr.add("pool", lambda e, src=src, parts=parts: e.tensor_tensor(parts[1], src, parts[0], ALU.subtract),
                                wait=[hi, scaled], done="w_low")

    ss = mem.bank(7, 2 * NC, B)
    for j in range(2 * NC):
        for k in range(NC):
            e1 = pr.add("pe", lambda e, j=j, k=k: e.matmul(ss[:, j], c.w_emb[:, k, j * P:(j + 1) * P], c.condT[:, :, k],
                                                           start=(k == 0), stop=(k == NC - 1)),
                        wait=[c.w_emb_in, c.small_in], done="emb" if j == 2 * NC - 1 and k == NC - 1 else None)
    c.w_emb_read = e1
    emb = mem.small("emb", 2 * NC, B)
    c.col_scale = mem.small("col_scale", NC, B)
    c.col_shift = emb[:, NC:]
    e2 = pr.add("dve", lambda e: e.tensor_tensor(emb[:], ss, c.b_emb[:].unsqueeze(2).broadcast_to([P, 2 * NC, B]), ALU.add),
                wait=[e1, c.small_in], done="prepared")
    c.emb_read = e2
    e3 = pr.add("dve", lambda e: e.tensor_scalar(c.col_scale[:], emb[:, :NC], 1.0, None, ALU.add), wait=[e2], done="prepared")
    c.col_done = pr.add("dve", lambda e: e.tensor_tensor(c.col_scale[:], c.col_scale[:],
                                                        c.g_norm[:].unsqueeze(2).broadcast_to([P, NC, B]), ALU.mult),
                        wait=[e3], done="prepared")


def top_k(pr, mem, c, during_search):
    v = mem.view("work", 0, FP32, B, NT, D)
    neg_max, total = mem.small("neg_max", B, NT), mem.small("total", B, NT)
    row_scale = mem.small("row_scale", B, NT)
    value = [None] * B
    for b in range(B):
        m = pr.add("dve", lambda e, b=b: e.tensor_reduce(neg_max[:, b], c.x[:, b], AX.X, ALU.max, negate=True),
                   wait=[c.x_in[b]], done="weighted")
        for t in range(NT):
            ex = pr.add("act", lambda e, b=b, t=t: e.activation(v[:, b, t], c.x[:, b, t], ACT.Exp, bias=neg_max[:, b, t:t + 1],
                                                                accum_out=total[:, b, t:t + 1]), wait=[m], done="exp_rows")
        r = pr.add("dve", lambda e, b=b: e.reciprocal(row_scale[:, b], total[:, b]), wait=[ex], done="weighted")
        r = pr.add("dve", lambda e, b=b: e.scalar_tensor_tensor(row_scale[:, b], row_scale[:, b], float(S) ** -0.5, c.fside[:, b],
                                                                ALU.mult, ALU.mult), wait=[r, c.fside_in], done="weighted")
        for t in range(NT):
            w = pr.add("dve", lambda e, b=b, t=t: e.scalar_tensor_tensor(v[:, b, t], v[:, b, t], row_scale[:, b, t:t + 1],
                                                                         c.cond_rows[:, b], ALU.mult, ALU.mult),
                       wait=[r, c.cond_in], done="weighted")
            value[b] = pr.add("pool", lambda e, b=b, t=t: e.affine_select(
                out=v[:, b, t, t * P:(t + 1) * P], in_=v[:, b, t, t * P:(t + 1) * P], compare_op=ALU.not_equal,
                fill=LOWEST, base=0, pattern=[[-1, P]], channel_multiplier=1), wait=[w, c.const], done="diagonal")

    c.cond_read = [w]
    N = S * D
    PER = NT * D
    flat = [v[:, b].rearrange("p t d -> p (t d)") for b in range(B)]
    keys = mem.view("w_b", 0, INT16, B, PER)
    lows = mem.view("w_b", 0, UINT16, B, PER)
    junk = mem.view("cols", 16, INT16, PER)
    junk_act = mem.view("cols", 20, INT16, PER)
    tally = mem.small("tally", B)
    tally_act = mem.small("tally_act", B)
    sign = mem.small("sign", B)
    rank = mem.small("rank", B)
    for b in range(B):
        t0 = pr.add("dve", lambda e, b=b: e.tensor_scalar(junk, flat[b], 0.0, 0.0, ALU.is_ge, ALU.add,
                                                          accum_out=tally[:, b:b + 1]),
                    wait=[value[b]] + ([("signed", pr.counts["signed"])] if b else []), done="signed")
    sums = mem.bank(6, B)
    q = pr.add("pe", lambda e: e.matmul(sums, c.ones[:], tally[:], start=True, stop=True), wait=[t0, c.const], done="sign_sum")
    enough = mem.small("enough", B)
    q = pr.add("dve", lambda e: e.tensor_scalar(enough[:], sums, float(TOPK), None, ALU.is_ge), wait=[q], done="signed")
    pr.add("dve", lambda e: e.tensor_scalar(sign[:], enough[:], 2.0, -1.0, ALU.mult, ALU.add), wait=[q], done="signed")
    q = pr.add("dve", lambda e: e.tensor_scalar(rank[:], enough[:], float(2 * TOPK - N - 1), float(N - TOPK + 1), ALU.mult, ALU.add),
               done="signed")
    turned = [None] * B
    for b in range(B):
        turned[b] = pr.add("dve", lambda e, b=b: e.tensor_scalar(flat[b], flat[b], sign[:, b:b + 1], 0.0, ALU.mult, ALU.add),
                           wait=[q], done="signed")

    ON_ACT = 7 * D // 2
    ON_DVE = PER - ON_ACT
    high = mem.small("high", B)
    low = mem.small("low", B)
    goal = mem.small("goal", B)
    bound = mem.small("bound", B)
    base = mem.small("base", B)
    passed = mem.small("passed", B)
    above = mem.small("above", B)

    def to_goal(ready, name):
        pr.add("dve", lambda e: e.tensor_copy(goal[:, 0:B:2], rank[:, 0:B:2]), wait=ready, done=name)
        return pr.add("dve", lambda e: e.tensor_scalar(goal[:, 1:B:2], rank[:, 1:B:2], -0.5 * P * ON_ACT, None, ALU.add), done=name)

    def count(g, data, ready, name):
        a, b = 2 * g, 2 * g + 1
        last_dve = dve_pass.get("at")
        pr.add("dve", lambda e: e.tensor_scalar(junk, data[:, a], bound[:, a:a + 1], 0.0, ALU.is_ge, ALU.add,
                                                accum_out=tally[:, a:a + 1]), wait=ready + [last_dve], done="count_dve")
        mine = ("count_dve", pr.counts["count_dve"])
        t1 = pr.add("dve", lambda e: e.tensor_scalar(junk[:, :ON_DVE], data[:, b, :ON_DVE], bound[:, b:b + 1], 0.0, ALU.is_ge,
                                                     ALU.add, accum_out=tally[:, b:b + 1]), wait=[mine], done="count_dve")
        dve_pass["at"] = t1
        t2 = pr.add("act", lambda e: e.activation(junk_act[:, :ON_ACT], data[:, b, ON_DVE:], ACT.Sign, scale=-1.0,
                                                  bias=bound[:, b:b + 1], accum_out=tally_act[:, b:b + 1]),
                    wait=ready + [dve_pass.get("act")], done="count_act")
        dve_pass["act"] = t2
        s = mem.bank(4 + g, 2)
        pr.add("pe", lambda e: e.matmul(s, c.ones[:], tally[:, a:b + 1], start=True, stop=False, skip_group_check=True),
               wait=[t1, dve_pass.get(("tested", g))])
        return pr.add("pe", lambda e: e.matmul(s[:, 1:2], c.minus_halves, tally_act[:, b:b + 1], start=False, stop=True,
                                               skip_group_check=True), wait=[t2], done=f"counted{g}")

    dve_pass = {}

    def descend(data, bits, ready, name):
        start = pr.add("dve", lambda e: e.memset(bound[:], 2.0 ** (bits - 1) - 0.5), wait=ready, done=name)
        at = [[start] + ready, [start] + ready]
        counted = [None, None]

        def update(g, bit):
            value, half = 2.0 ** bit, 2.0 ** (bit - 1)
            cols = slice(2 * g, 2 * g + 2)
            b0 = pr.add("dve", lambda e, cols=cols, d=(-value + half if bit else -value): e.tensor_scalar(
                base[:, cols], bound[:, cols], d, None, ALU.add), wait=at[g], done=name)
            t = pr.add("dve", lambda e, g=g, cols=cols: e.tensor_tensor(passed[:, cols], mem.bank(4 + g, 2), goal[:, cols], ALU.is_ge),
                       wait=[counted[g]], done=name)
            dve_pass["tested", g] = t
            at[g] = [pr.add("dve", lambda e, cols=cols, value=value: e.scalar_tensor_tensor(
                bound[:, cols], passed[:, cols], value, base[:, cols], ALU.mult, ALU.add), wait=[t, b0], done=name)]

        counted[0] = count(0, data, at[0], name)
        for bit in reversed(range(bits)):
            counted[1] = count(1, data, at[1], name)
            update(0, bit)
            if bit:
                counted[0] = count(0, data, at[0], name)
            update(1, bit)
        return at[0] + at[1]

    halves = [f.bitcast(INT16).rearrange("p (n two) -> p n two", two=2) for f in flat]
    uhalves = [f.bitcast(UINT16).rearrange("p (n two) -> p n two", two=2) for f in flat]
    for b in range(B):
        eng = "act" if b % 2 else "pool"
        if eng == "act":
            k = pr.add("act", lambda e, b=b: e.activation(keys[:, b], halves[b][:, :, 1], ACT.Copy), wait=[turned[b]], done="keys_act")
        else:
            k2 = pr.add("pool", lambda e, b=b: e.tensor_copy(keys[:, b], halves[b][:, :, 1]), wait=[turned[b]], done="keys_pool")
    during_search()
    gl = to_goal([q], "search")
    hs = descend(keys, 15, [k, k2, gl], "search")
    h = pr.add("dve", lambda e: e.tensor_scalar(high[:], bound[:], 0.5, None, ALU.add), wait=hs, done="search")
    ab = pr.add("dve", lambda e: e.tensor_scalar(base[:], high[:], 0.5, None, ALU.add), wait=[h], done="search")
    for b in range(B):
        a1 = pr.add("dve", lambda e, b=b: e.tensor_scalar(junk, keys[:, b], base[:, b:b + 1], 0.0, ALU.is_ge, ALU.add,
                                                          accum_out=tally[:, b:b + 1]),
                    wait=[ab, dve_pass["at"]] + ([("search", pr.counts["search"])] if b else []), done="search")
    a2 = pr.add("pe", lambda e: e.matmul(sums, c.ones[:], tally[:], start=True, stop=True), wait=[a1], done="above_sum")
    a3 = pr.add("dve", lambda e: e.tensor_tensor(rank[:], rank[:], sums, ALU.subtract), wait=[a2], done="search")
    for b in range(B):
        lw = pr.add("dve", lambda e, b=b: e.scalar_tensor_tensor(lows[:, b], keys[:, b], high[:, b:b + 1], uhalves[b][:, :, 0],
                                                                 ALU.is_equal, ALU.mult), wait=[a1, h], done="lows")
    gl = to_goal([a3], "search")
    ls = descend(lows, 16, [lw, gl], "search")

    pivot = mem.small("pivot", B)
    neg_pivot = mem.small("neg_pivot", B)
    whole = pivot[:].bitcast(INT16).rearrange("p (n two) -> p n two", two=2)
    uwhole = pivot[:].bitcast(UINT16).rearrange("p (n two) -> p n two", two=2)
    l = pr.add("dve", lambda e: e.tensor_scalar(low[:], bound[:], 0.5, None, ALU.add), wait=ls, done="search")
    pr.add("dve", lambda e: e.tensor_copy(whole[:, :, 1], high[:]), wait=[l], done="search")
    pz = pr.add("dve", lambda e: e.tensor_copy(uwhole[:, :, 0], low[:]), done="search")
    eq = mem.view("w_b", 0, FP16, NT, D)
    prefix = mem.view("w_b", 4, FP32, NT, D)
    taken = mem.view("w_b", 12, FP16, NT, D)
    zeros = mem.view("w_b", 16, FP32, D)
    zz = pr.add("pool", lambda e: e.memset(zeros, 0.0), wait=ls, done="zeros")
    n_eq = mem.small("n_eq", B, NT)
    n_gt = mem.small("n_gt", B)
    gt_sign = mem.small("gt_sign", B)
    pv = pr.add("dve", lambda e: e.tensor_tensor(pivot[:], pivot[:], sign[:], ALU.mult), wait=[pz], done="search")
    npv = pr.add("dve", lambda e: e.tensor_scalar(neg_pivot[:], pivot[:], -1.0, None, ALU.mult), wait=[pv], done="search")
    back = [None] * B
    for b in range(B):
        back[b] = pr.add("dve", lambda e, b=b: e.tensor_scalar(flat[b], flat[b], sign[:, b:b + 1], None, ALU.mult), wait=[lw], done="search")
    gt = [pr.add("act", lambda e, b=b: e.activation(junk_act, flat[b], ACT.Sign, bias=neg_pivot[:, b:b + 1],
                                                    accum_out=gt_sign[:, b:b + 1]),
                 wait=[back[b], npv] + ([("gt_sign", pr.counts["gt_sign"])] if b else [dve_pass["act"]]), done="gt_sign") for b in range(B)]
    earlier = mem.small("earlier", B, NT)
    quota = mem.small("quota", B, NT)
    row_eq = mem.small("row_eq", B)
    places = mem.bank(6, B, NT)
    c.x1 = [None] * B
    prev_taken = None
    prev_sel = None
    qdone = None
    zero_earlier = pr.add("dve", lambda e: e.memset(earlier[:, :, 0:1], 0.0), done="quota")
    for b in range(B):
        for t in range(NT):
            ee = pr.add("dve", lambda e, b=b, t=t: e.tensor_scalar(eq[:, t], v[:, b, t], pivot[:, b:b + 1], 0.0, ALU.is_equal, ALU.add,
                                                                   accum_out=n_eq[:, b, t:t + 1]),
                        wait=[back[b], pv, prev_sel] + ls, done="equal")
        for t in range(1, NT):
            er = pr.add("dve", lambda e, b=b, t=t: e.tensor_tensor(earlier[:, b, t:t + 1], earlier[:, b, t - 1:t], n_eq[:, b, t - 1:t], ALU.add),
                        wait=[ee, zero_earlier] + ([er] if t > 1 else []), done="quota")
        er = pr.add("dve", lambda e, b=b: e.tensor_tensor(row_eq[:, b:b + 1], earlier[:, b, NT - 1:NT], n_eq[:, b, NT - 1:NT], ALU.add),
                    wait=[er], done="quota")
        er = pr.add("dve", lambda e, b=b: e.tensor_scalar(n_gt[:, b:b + 1], gt_sign[:, b:b + 1], row_eq[:, b:b + 1], float(PER), ALU.subtract, ALU.add),
                    wait=[er, gt[b]], done="quota")
        er = pr.add("dve", lambda e, b=b: e.scalar_tensor_tensor(earlier[:, b], n_gt[:, b:b + 1].broadcast_to([P, NT]), 0.5, earlier[:, b], ALU.mult, ALU.add),
                    wait=[er], done="quota")
        pr.add("pe", lambda e, b=b: e.matmul(places[:, b], c.before, n_eq[:, b], start=True, stop=False), wait=[ee, a3, qdone])
        pl = pr.add("pe", lambda e, b=b: e.matmul(places[:, b], c.ones[:], earlier[:, b], start=False, stop=True), wait=[er], done="places")
        qu = pr.add("dve", lambda e, b=b: e.tensor_scalar(quota[:, b], places[:, b], -1.0, float(TOPK), ALU.mult, ALU.add), wait=[pl], done="quota")
        qdone = c.places_read = qu
        for t in range(NT):
            sc = pr.add("dve", lambda e, b=b, t=t: e.tensor_tensor_scan(prefix[:, t], eq[:, t], zeros, 0.0, ALU.add, ALU.add),
                        wait=[ee, zz, prev_taken], done="prefix")
            sl = pr.add("dve", lambda e, b=b, t=t: e.scalar_tensor_tensor(taken[:, t], prefix[:, t], quota[:, b, t:t + 1], eq[:, t], ALU.is_le, ALU.mult),
                        wait=[sc, qu, prev_taken], done="taken")
            ga = pr.add("dve", lambda e, b=b, t=t: e.scalar_tensor_tensor(c.x[:, b, t], v[:, b, t], pivot[:, b:b + 1], c.x[:, b, t], ALU.is_gt, ALU.add),
                        done="greater")
            c.x1[b] = pr.add("pool", lambda e, b=b, t=t: e.tensor_tensor(c.x[:, b, t], c.x[:, b, t], taken[:, t], ALU.add), wait=[sl, ga], done="masked")
        prev_taken = c.x1[b]
        prev_sel = sl


def scale_of(pr, mem, name, most, ready, engine_name):
    absmax, power, scale, unscale = (mem.small(f"{name}_{x}", 1) for x in ("absmax", "power", "scale", "unscale"))
    r = pr.add("pool", lambda e: e.partition_all_reduce(absmax[:], most, P, bass.bass_isa.ReduceOp.max), wait=[ready], done="absmax")
    r = pr.add("dve", lambda e: e.tensor_scalar(absmax[:], absmax[:], 2.0 ** -60, None, ALU.max), wait=[r], done=engine_name)
    p = power_of_two(pr, engine_name, power[:], absmax[:], [r])
    r = pr.add("dve", lambda e: e.reciprocal(scale[:], power[:]), wait=[p], done=engine_name)
    pr.add("dve", lambda e: e.tensor_scalar(unscale[:], power[:], 2.0 ** -13, None, ALU.mult), done=engine_name)
    return scale, unscale, pr.add("dve", lambda e: e.tensor_scalar(scale[:], scale[:], 2.0 ** 13, None, ALU.mult), wait=[r], done=engine_name)


def input_weights(pr, mem, c, w_a_free):
    c.w_ih16 = mem.view("w_a", 0, FP16, 2, NC, GATES * D)
    chunk_most = mem.small("ih_chunk_most", NC + 1)
    jobs = []
    for k in range(NC):
        def largest(k=k):
            c.ih_most = pr.add("dve", lambda e: e.tensor_reduce(chunk_most[:, k:k + 1], c.w_ih[:, k], AX.X, ALU.max, apply_absolute_value=True),
                               wait=[c.w_ih_in], done="ih_most")
        jobs.append(largest)

    def scale():
        m = pr.add("dve", lambda e: e.tensor_reduce(chunk_most[:, NC:], chunk_most[:, :NC], AX.X, ALU.max), wait=[c.ih_most], done="ih_most")
        c.ih_scale, c.ih_unscale, c.ih_scaled = scale_of(pr, mem, "ih", chunk_most[:, NC:], m, "ih_scale")
    jobs.append(scale)
    for k in range(NC):
        for g in range(GATES):
            def parts(k=k, g=g):
                cols = slice(g * D, (g + 1) * D)
                w = c.w_ih[:, k, cols]
                sc = pr.add("pool", lambda e: e.tensor_tensor(w, w, c.ih_scale[:].broadcast_to([P, D]), ALU.mult), wait=[c.ih_scaled], done="ih_parts")
                hi = pr.add("pool", lambda e: e.tensor_copy(c.w_ih16[:, 0, k, cols], w), wait=[sc, w_a_free], done="ih_parts")
                c.w_ih16_done = pr.add("pool", lambda e: e.tensor_tensor(c.w_ih16[:, 1, k, cols], w, c.w_ih16[:, 0, k, cols], ALU.subtract),
                                       wait=[hi], done="ih_parts")
            jobs.append(parts)
    return jobs


def attention(pr, mem, c, w_ih, cond):
    squares = mem.view("cols", 16, FP32, D)
    power = mem.small("row_power", B, NT)
    row_rms = mem.small("row_rms", B, NT)
    for b in range(B):
        for t in range(NT):
            sq = pr.add("act", lambda e, b=b, t=t: e.activation(squares, c.x[:, b, t], ACT.Square, accum_out=power[:, b, t:t + 1]),
                        wait=[c.x1[b]] + ([sq] if b + t else []), done="row_power")
    m = pr.add("dve", lambda e: e.tensor_scalar(row_rms[:], power[:], 1.0 / D, EPS, ALU.mult, ALU.add), wait=[sq], done="inverse_rms")
    m = pr.add("act", lambda e: e.activation(row_rms[:], row_rms[:], ACT.Sqrt), wait=[m], done="row_root")
    rms = pr.add("dve", lambda e: e.reciprocal(row_rms[:], row_rms[:]), wait=[m], done="inverse_rms")

    c.xT = mem.view("cols", 0, FP32, NC, B, S)
    QK = 2 * HEADS
    diagonal = mem.view("work", 24, FP32, NT, P)
    qk = mem.view("work", 0, FP32, NT, QK, DH)
    sq_qk = mem.view("work", 24, FP32, QK, DH)
    stacks_of = [[mem.view("work", 28, FP16, HEADS, 4, DH), mem.view(*place, FP16, HEADS, 4, DH)]
                 for place in (("cond", 0), ("rows", 0), ("rows", 8), ("rows", 16))]
    probT = mem.view("work", 0, FP32, HPG, NT, S)
    xnT = mem.view("work", 16, FP32, NC, S)
    qT = mem.view("scratch", 0, FP16, HEADS, S)
    kT = mem.view("w_b", 0, FP16, HEADS, S)
    v = mem.view("w_b", 16, FP32, NT, D)
    oT = mem.view("cond", 0, FP32, NC, S)
    head_power = mem.small("head_power", NT, QK)
    top = mem.small("top", NT * HEADS)
    neg_top = mem.small("neg_top", NT * HEADS)
    weight = mem.small("weight", NT, HEADS)
    inv_weight = mem.small("inv_weight", NT, HPG)
    last = {}
    bank_read = [c.places_read] * 8
    out_done = None

    def columns_of(b):
        for t in range(NT):
            dg = pr.add("dve", lambda e, t=t: e.tensor_scalar(diagonal[:, t], c.ident[:], row_rms[:, b, t:t + 1], None, ALU.mult),
                        wait=[rms, last.get("pv"), c.x1[B - 1]], done="diagonals")
        for k in range(NC):
            raw_bank, nrm_bank = k % 2, 2 + k % 2
            raw, nrm = mem.bank(raw_bank, S), mem.bank(nrm_bank, S)
            for t in range(NT):
                e1 = pr.add("pe", lambda e, k=k, t=t, raw=raw: e.transpose(raw[:, t * P:(t + 1) * P], c.x[:, b, t, k * P:(k + 1) * P], c.ident[:]),
                            wait=[c.x1[b], bank_read[raw_bank], c.w_emb_read], done="x_turned" if t == NT - 1 else None)
            for t in range(NT):
                e2 = pr.add("pe", lambda e, k=k, t=t, nrm=nrm: e.matmul(nrm[:, t * P:(t + 1) * P], c.x[:, b, t, k * P:(k + 1) * P], diagonal[:, t],
                                                                        start=True, stop=True),
                            wait=[dg, bank_read[nrm_bank]], done="normed_turned" if t == NT - 1 else None)
            xc = bank_read[raw_bank] = pr.add("dve", lambda e, k=k, raw=raw: e.tensor_copy(c.xT[:, k, b], raw), wait=[e1, rms, c.w16_done], done="x_cols")
            xn = bank_read[nrm_bank] = pr.add("act", lambda e, k=k, nrm=nrm: e.activation(
                xnT[:, k], nrm, ACT.Identity, scale=c.col_scale[:, k, b:b + 1], bias=c.col_shift[:, k, b:b + 1]),
                wait=[e2, c.col_done, last.get("pv")], done="x_normed_cols")
        return e1, e2, xc, xn

    c.x_most = mem.small("x_most", B * NC)

    def out_matmuls(ready):
        made = []
        for m in range(NC):
            for k in range(NC):
                wo = pr.add("pe", lambda e, m=m, k=k: e.matmul(mem.bank(m, S), c.w_out[:, k, m * P:(m + 1) * P], oT[:, k],
                                                             start=(k == 0), stop=(k == NC - 1)),
                            wait=[ready, c.w_out_in, bank_read[m]], done="w_out" if k == NC - 1 else None)
            made.append(wo)
        last["w_out"] = wo
        return made

    def out_adds(b, made, ready, xc):
        for m in range(NC):
            last["plus"] = pr.add("pool", lambda e, m=m: e.tensor_tensor(c.xT[:, m, b], c.xT[:, m, b], oT[:, m], ALU.add),
                                  wait=[ready, xc], done="plus_o")
            last["x2"] = bank_read[m] = pr.add("dve", lambda e, m=m: e.tensor_tensor(c.xT[:, m, b], c.xT[:, m, b], mem.bank(m, S), ALU.add),
                                               wait=[made[m], last["plus"]], done="plus_w_out")
            c.x_most_done = pr.add("dve", lambda e, m=m: e.tensor_reduce(c.x_most[:, b * NC + m:b * NC + m + 1], c.xT[:, m, b], AX.X, ALU.max,
                                                                        apply_absolute_value=True), wait=[last["x2"]], done="x_most")

    columns = columns_of(0)
    for b in range(B):
        probs = mem.view("rows", 8 * b, FP32, 4, S)
        xc_before = xc if b else None
        e1, e2, xc, xn = columns
        made_of = {}

        def project(t, outputs=(0, 1, 2)):
            banks = [3 * (t % 2) + i for i in range(3)]
            made = made_of.setdefault(t, [None] * 3)
            for i in outputs:
                for k in range(NC):
                    made[i] = pr.add("pe", lambda e, i=i, k=k, t=t, banks=banks: e.matmul(
                        mem.bank(banks[i], D), xnT[:, k, t * P:(t + 1) * P], c.w_qkv[:, k, i * D:(i + 1) * D],
                        start=(k == 0), stop=(k == NC - 1)), wait=[xn, c.w_qkv_in, bank_read[banks[i]]],
                        done="projected" if k == NC - 1 else None)
            last["projected"] = made[2]
            return banks, made

        def take_projected(t, banks, made):
            for i in range(2):
                sq = pr.add("act", lambda e, i=i, banks=banks: e.activation(
                    sq_qk[:, i * HEADS:(i + 1) * HEADS], mem.bank(banks[i], HEADS, DH), ACT.Square),
                    wait=[made[i], e2, last.get("sq_read"), last.get("pv"), rms], done="qk_square")
                last["copied"] = bank_read[banks[i]] = pr.add("act", lambda e, i=i, t=t, banks=banks: e.activation(
                    qk[:, t, i * HEADS:(i + 1) * HEADS], mem.bank(banks[i], HEADS, DH), ACT.Copy), done="qk_rows")
            last["sq_read"] = hp = pr.add("dve", lambda e, t=t: e.tensor_reduce(head_power[:, t], sq_qk, AX.X, ALU.add),
                                          wait=[sq, last.get("heads_read")], done="head_power")
            last["values"] = bank_read[banks[2]] = pr.add("dve", lambda e, t=t, banks=banks: e.tensor_copy(v[:, t], mem.bank(banks[2], D)),
                                                          wait=[made[2], last.get("pv")], done="values")
            m = pr.add("dve", lambda e, t=t: e.tensor_scalar(head_power[:, t], head_power[:, t], 1.0 / DH, EPS, ALU.mult, ALU.add),
                       wait=[hp], done="inverse_rms")
            m = pr.add("act", lambda e, t=t: e.activation(head_power[:, t], head_power[:, t], ACT.Sqrt), wait=[m], done="head_root")
            return pr.add("dve", lambda e, t=t: e.reciprocal(head_power[:, t], head_power[:, t]), wait=[m], done="inverse_rms")

        def norm_heads(t, m):
            n = pr.add("dve", lambda e, t=t: e.tensor_tensor(qk[:, t], qk[:, t], head_power[:, t].unsqueeze(2).broadcast_to([P, QK, DH]), ALU.mult),
                       wait=[m, last["copied"]], done="qk_normed")
            last["heads_read"] = n
            keyed = pr.add("pool", lambda e, t=t: e.tensor_tensor(
                qk[:, t, HEADS:], qk[:, t, HEADS:], c.gain[:].unsqueeze(1).broadcast_to([P, HEADS, DH]), ALU.mult),
                wait=[n, c.gain_done], done="keys_gained")
            return n, keyed

        def stack_parts(t, i, n, keyed):
            stack = stacks_of[b][i]
            src = qk[:, t, i * HEADS:(i + 1) * HEADS].unsqueeze(2).broadcast_to([P, HEADS, 2, DH])
            hi = stack[:, :, 0:2] if i == 0 else stack[:, :, 0:4:2]
            lo = stack[:, :, 2:4] if i == 0 else stack[:, :, 1:4:2]
            s1 = pr.add("act", lambda e, src=src, hi=hi: e.activation(hi, src, ACT.Copy),
                        wait=[n if i == 0 else keyed, last.get(("stack_read", i)), last.get("pv")] + c.cond_read, done="stack_high")
            for slot in range(2):
                s2 = pr.add("dve", lambda e, i=i, t=t, hi=hi, lo=lo, slot=slot: e.tensor_tensor(
                    lo[:, :, slot], qk[:, t, i * HEADS:(i + 1) * HEADS], hi[:, :, slot], ALU.subtract),
                    wait=[s1, keyed], done="stack_low")
            return s2

        def turn_stack(t, i, s2):
            stack = stacks_of[b][i]
            for half in range(2):
                bk = 6 + half
                to = mem.banks[bk][:].bitcast(FP16).rearrange("p (h n) -> p h n", h=8)
                for h in range(8):
                    tp = pr.add("pe", lambda e, to=to, h=h, half=half, stack=stack: e.transpose(
                        to[:, h], stack[:, half * 8 + h].rearrange("p a d -> p (a d)"), c.ident16[:]),
                        wait=[s2, bank_read[bk]], done="stack_turned" if h == 7 else None)
                dst = (qT if i == 0 else kT)[:, half * 8:half * 8 + 8, t * P:(t + 1) * P]
                w = [tp, last.get("scores"), xc]
                if half == 0:
                    bank_read[bk] = pr.add("act", lambda e, to=to, dst=dst: e.activation(dst, to, ACT.Copy), wait=w, done="heads_act")
                else:
                    bank_read[bk] = pr.add("dve", lambda e, to=to, dst=dst: e.tensor_copy(dst, to), wait=w, done="heads_dve")
            last["stack_read", i] = tp

        head_rms = take_projected(0, *project(0))
        keys_ready = None
        for t in range(1, NT):
            project(t, (0,))
            if keys_ready:
                turn_stack(t - 2, 1, keys_ready)
            projected = project(t, (1, 2))
            normed = norm_heads(t - 1, head_rms)
            turn_stack(t - 1, 0, stack_parts(t - 1, 0, *normed))
            keys_ready = stack_parts(t - 1, 1, *normed)
            head_rms = take_projected(t, *projected)
        out = out_matmuls(oT_ready) if b else None
        turn_stack(NT - 2, 1, keys_ready)
        normed = norm_heads(NT - 1, head_rms)
        ready = [stack_parts(NT - 1, i, *normed) for i in range(2)]
        for i in range(2):
            turn_stack(NT - 1, i, ready[i])
        if b:
            out_adds(b - 1, out, oT_ready, xc_before)
            out_done = last["w_out"]
        weight_jobs = []
        if b == B - 1:
            c.w_ih = mem.view("rows", 0, FP32, NC, GATES * D)
            c.w_ih_in = pr.dma("sp", c.w_ih, w_ih.rearrange("(k p) n -> p k n", p=P), "w_ih_in", wait=[last["stack_read", 1], last["pv"]])
            weight_jobs = input_weights(pr, mem, c, last["projected"])
        heads_made = [bank_read[6], bank_read[7]]

        def scores(g, t, pair):
            bks = [2 * pair, 2 * pair + 1]
            col = t * HEADS + g * HPG + 2 * pair
            scored = []
            for i in range(2):
                h = g * HPG + 2 * pair + i
                scored.append(pr.add("pe", lambda e, i=i, h=h, t=t, bks=bks: e.matmul(
                    mem.bank(bks[i], S), qT[:, h, t * P:(t + 1) * P], kT[:, h], start=True, stop=True),
                    wait=heads_made + [bank_read[bks[i]]], done="scores"))
            last["scores"] = scored[1]
            for i in range(2):
                mx = pr.add("dve", lambda e, i=i, bks=bks, col=col: e.tensor_reduce(
                    top[:, col + i:col + i + 1], mem.bank(bks[i], S), AX.X, ALU.max), wait=[scored[i], last.get(("exp", b - 1))], done="top")
            return pr.add("dve", lambda e, col=col: e.tensor_scalar(neg_top[:, col:col + 2], top[:, col:col + 2], c.minus_logit_scale[:], None, ALU.mult),
                          wait=[mx, c.gain_done], done="neg_top")

        def exponentials(g, t, pair, nm):
            bks = [2 * pair, 2 * pair + 1]
            col = t * HEADS + g * HPG + 2 * pair
            made = []
            for i in range(2):
                h = g * HPG + 2 * pair + i
                slot = 2 * pair + i
                ex = bank_read[bks[i]] = pr.add("act", lambda e, i=i, h=h, t=t, slot=slot, bks=bks, col=col, probs=probs: e.activation(
                    probs[:, slot], mem.bank(bks[i], S), ACT.Exp, scale=c.logit_scale[:], bias=neg_top[:, col + i:col + i + 1],
                    accum_out=weight[:, t, h:h + 1]), wait=[nm, e1, e2, last.get(("turned", slot)), last.get("weights_read")], done="exp")
                made.append(ex)
            last["exp", b] = last["exp"] = ex
            return made

        def turn(g, t, pair, made):
            for i in range(2):
                slot, bk = 2 * pair + i, 4 + i
                for kt in range(NT):
                    tp = pr.add("pe", lambda e, kt=kt, slot=slot, bk=bk, probs=probs: e.transpose(
                        mem.bank(bk, NT, P)[:, kt], probs[:, slot, kt * P:(kt + 1) * P], c.ident[:]),
                        wait=[made[i], bank_read[bk]], done="probs_turned" if kt == NT - 1 else None)
                last["turned", slot] = tp
                dst = probT[:, 2 * pair + i, :, t * P:(t + 1) * P]
                w = [tp, last.get("pv") if b and g == 0 else last.get(("pv", t // 2))]
                if i == 0:
                    bank_read[bk] = pr.add("act", lambda e, bk=bk, dst=dst: e.activation(dst, mem.bank(bk, NT, P), ACT.Copy), wait=w, done="probs_act")
                else:
                    bank_read[bk] = pr.add("dve", lambda e, bk=bk, dst=dst: e.tensor_copy(dst, mem.bank(bk, NT, P)), wait=w, done="probs_dve")

        def weighted_values(g, half, kt):
            queries = slice(half * 2 * P, (half + 1) * 2 * P)
            for i in range(HPG):
                h = g * HPG + i
                pv = pr.add("pe", lambda e, i=i, h=h: e.matmul(
                    mem.banks[6][DH * i:DH * i + DH, queries], v[:, kt, h * DH:(h + 1) * DH], probT[:, i, kt, queries],
                    start=(kt == 0), stop=(kt == NT - 1), tile_position=(0, DH * i)),
                    wait=[probs_turned[half], probs_turned[half, 1], bank_read[6], last["values"]],
                    done="pv" if kt == NT - 1 and i == HPG - 1 else None)
            if kt == NT - 1:
                last["pv"] = last["pv", half] = pv

        def spread_inverse(g, made):
            iv = pr.add("dve", lambda e, g=g: e.reciprocal(inv_weight[:], weight[:, :, g * HPG:(g + 1) * HPG]),
                        wait=[made[1], last.get("inv_spread")], done="inv_weight")
            last["weights_read"] = iv if g == NC - 1 else last.get("weights_read")
            spread = oT[:, g].rearrange("p (t h d) -> p t h d", t=NT, h=HPG)
            source = inv_weight[:].unsqueeze(3).broadcast_to([P, NT, HPG, DH])
            waits = [iv, last["projected"], out_done, last.get("plus"), last["stack_read", 1]]
            if b == B - 1:
                sp = pr.add("act", lambda e: e.activation(spread, source, ACT.Copy), wait=waits, done="inv_spread_act")
            else:
                sp = pr.add("pool", lambda e: e.tensor_copy(spread, source), wait=waits, done="inv_spread")
            last["inv_spread"] = sp
            return sp

        def divide(g, sp):
            for t in range(NT):
                ic = pr.add("pe", lambda e, g=g, t=t: e.matmul(
                    mem.bank(7, S)[:, t * P:(t + 1) * P], oT[:, g, t * P:(t + 1) * P],
                    c.ident[:], start=True, stop=True), wait=[sp, bank_read[7]], done="inv_turned" if t == NT - 1 else None)
            cpi = bank_read[7] = pr.add("act", lambda e, g=g: e.activation(oT[:, g], mem.bank(7, S), ACT.Copy),
                                        wait=[ic], done="inv_cols")
            last["out_scaled"] = bank_read[6] = pr.add("dve", lambda e, g=g: e.tensor_tensor(oT[:, g], mem.bank(6, S), oT[:, g], ALU.mult),
                                                       wait=[last["pv"], cpi, out_done] + c.cond_read, done="out_cols")

        units = [(g, t, pair) for g in range(NC) for t in range(NT) for pair in range(2)]
        ahead = 2
        probs_turned, todo = {}, []
        made = [exponentials(*u, scores(*u)) for u in units[:ahead]]
        for n_, unit in enumerate(units):
            now = made.pop(0)
            coming = units[n_ + ahead] if n_ + ahead < len(units) else None
            nm = scores(*coming) if coming else None
            if todo:
                todo.pop(0)()
            turn(*unit, now)
            g, t, pair = unit
            if t % 2 == 1 and pair == 1:
                probs_turned[t // 2], probs_turned[t // 2, 1] = bank_read[4], bank_read[5]
                todo += [lambda g=g, half=t // 2, kt=kt: weighted_values(g, half, kt) for kt in range(NT)]
                if t == NT - 1:
                    final, ic = todo.pop(), spread_inverse(g, now)
                    todo.append(lambda g=g, ic=ic, final=final: (final(), divide(g, ic)))
            if coming:
                made.append(exponentials(*coming, nm))
            if weight_jobs and n_ >= 6:
                weight_jobs.pop(0)()
        for job in todo:
            job()
        if b + 1 < B:
            columns = columns_of(b + 1)
        oT_ready = last["out_scaled"]
        if b == B - 1:
            out_adds(b, out_matmuls(oT_ready), oT_ready, xc)
            a1, a2, wo = last["plus"], last["x2"], last["w_out"]
    c.x2 = [a2]
    c.attention_over = [a2, wo, a1, last["out_scaled"], last["pv"], last["scores"]]
    c.bank_read = bank_read


def floor_and_weights(pr, mem, c, cond):
    grid = mem.view("cond", 0, FP32, B, D)
    whole = mem.view("w_b", 0, FP32, B, D)
    as_int = mem.view("w_b", 8, INT32, B, D)
    w0 = mem.view("w_b", 8, FP32, B, D)
    right = mem.view("w_b", 16, FP32, B, D)
    c.sampling = mem.view("rows", 0, FP32, B, NC, D)
    part = mem.view("scratch", 12, FP32, 2, D)
    loaded = pr.dma("sp", grid.rearrange("p b d -> p (b d)"), cond.rearrange("b d -> (b d)").partition_broadcast(P),
                    "grid_in", wait=c.attention_over)

    far = 2.0 ** 24
    state = {"at": loaded, "right_read": None}

    def dve(emit, *wait):
        state["at"] = pr.add("dve", emit, wait=[state["at"]] + list(wait), done="grid")
        return state["at"]

    jobs = []
    for b in range(B):
        place, fl, integer, left, nxt = grid[:, b], whole[:, b], as_int[:, b], w0[:, b], right[:, b]
        jobs += [
            lambda place=place: dve(lambda e: e.tensor_scalar(place, place, 1.0, 0.5, ALU.add, ALU.mult), *c.attention_over),
            lambda place=place: dve(lambda e: e.tensor_scalar(place, place, float(D - 1), far, ALU.mult, ALU.min)),
            lambda place=place: dve(lambda e: e.tensor_scalar(place, place, -far, None, ALU.max)),
            lambda place=place, integer=integer: dve(lambda e: e.tensor_copy(integer, place)),
            lambda fl=fl, integer=integer: dve(lambda e: e.tensor_copy(fl, integer)),
            lambda fl=fl, nxt=nxt, place=place: dve(lambda e: e.tensor_tensor(nxt, fl, place, ALU.is_gt)),
            lambda fl=fl, nxt=nxt: dve(lambda e: e.tensor_tensor(fl, fl, nxt, ALU.subtract)),
            lambda fl=fl, place=place: dve(lambda e: e.tensor_tensor(place, place, fl, ALU.subtract)),
            lambda left=left, place=place: dve(lambda e: e.tensor_scalar(left, place, -1.0, 1.0, ALU.mult, ALU.add)),
            lambda nxt=nxt, fl=fl: dve(lambda e: e.tensor_scalar(nxt, fl, 1.0, 0.0, ALU.add, ALU.max)),
            lambda nxt=nxt: dve(lambda e: e.tensor_scalar(nxt, nxt, float(D - 1), None, ALU.min)),
            lambda fl=fl: dve(lambda e: e.tensor_scalar(fl, fl, 0.0, float(D - 1), ALU.max, ALU.min))]
        for k in range(NC):
            def left_job(b=b, k=k):
                dve(lambda e: e.scalar_tensor_tensor(
                    c.sampling[:, b, k], whole[:, b], c.feature[:, k:k + 1], w0[:, b], ALU.is_equal, ALU.mult), c.w_ih_read)

            def right_job(b=b, k=k):
                to, slot = c.sampling[:, b, k], k % 2
                r = dve(lambda e: e.scalar_tensor_tensor(
                    part[:, slot], right[:, b], c.feature[:, k:k + 1], grid[:, b], ALU.is_equal, ALU.mult), read[slot])
                read[slot] = s = pr.add("pool", lambda e: e.tensor_tensor(to, to, part[:, slot], ALU.add), wait=[r], done="sampling")
                diagonal = to[:, k * P:(k + 1) * P]
                c.sampling_done[b] = pr.add("pool", lambda e: e.tensor_tensor(diagonal, diagonal, c.ident[:], ALU.add),
                                            wait=[s], done="sampling")
            jobs += [left_job, right_job]
    read = [None, None]
    c.sampling_done = [None] * B
    return jobs


STEPS_PER_CHUNK = 32
GROUP = 4
UNITS = "ABz AAn AAr AAz BAr BAz BAn ABr BBr BBz ABn BBn".split()
ORDER = ("rsumA zsumA rsigA zaddA nmulA zsigA nsumA tanhA omzA rsumB zhA rsigB zsumB tmulA zsplitA nputA zaddB "
         "nmulB zsigB tlowA nsumB tanhB omzB stateA zlowA zhB tmulB tlowB rputA zsplitB zlowB rputB stateB nputB").split()


def gru(pr, mem, c, jobs, out):
    state = mem.view("work", 0, FP32, S + 1, NC, B)
    gates_in = mem.view("scratch", 0, FP32, 2, 2 * GATES * 2, B, STEPS_PER_CHUNK)
    bias_in = mem.small("bias_in", 2, GATES, 2)
    n_bias = mem.small("n_bias", 2, 2)
    parts = [[mem.small(f"parts{parity}{half}", 2, 4, B, dtype=FP16) for half in "AB"] for parity in range(2)]
    rz = [mem.small(f"rz{h}", 4, B) for h in "AB"]
    gate = [mem.small(f"gate{h}", 4, B) for h in "AB"]
    nm = [mem.small(f"nm{h}", 2, 6, B) for h in "AB"]
    nsum = [mem.small(f"nsum{h}", 2, B) for h in "AB"]
    new = [mem.small(f"new{h}", 2, B) for h in "AB"]
    one_minus_z = [mem.small(f"one_minus_z{h}", 2, B) for h in "AB"]
    t_ = [mem.small(f"t{h}", 2, B) for h in "AB"]
    zh = [mem.small(f"zh{h}", 2, B) for h in "AB"]
    rows_out = mem.view("w_b", 0, FP32, 4, D)
    r_bank, z_bank, n_bank, side_bank = (0, 1), (2, 3), (4, 5), (6, 7)

    def of_bank(bank):
        return mem.bank(bank, 2, 5, B)

    over = c.attention_over
    both = mem.small("both", GATES, NC)
    for half in range(2):
        cleared = pr.add("pool", lambda e, half=half: e.memset(parts[0][half][:], 0.0), done="gru_ready")
    pr.add("dve", lambda e: e.tensor_copy(both[:], c.b_ih[:]), wait=[c.small_in, c.scale], done="gru_first")
    bi = ("gru_first", pr.counts["gru_first"])
    bi = pr.add("dve", lambda e: e.tensor_tensor(both[:, :2], c.b_ih[:, :2], c.b_hh[:, :2], ALU.add), wait=[bi], done="gru_first")
    bi = pr.add("dve", lambda e: e.tensor_scalar(bias_in[:].rearrange("p m g c -> p g m c"), both[:].rearrange("p g (m c) -> p g m c", c=2),
                                                 c.gate_scale[:], None, ALU.mult), wait=[bi], done="gru_first")
    for half in range(2):
        pr.add("dve", lambda e, half=half: e.tensor_scalar(
            of_bank(n_bank[half])[:, :, 4], c.b_hh[:, 2, 2 * half:2 * half + 2].unsqueeze(2).broadcast_to([P, 2, B]), c.gate_scale[:], None, ALU.mult),
            wait=[c.bank_read[n_bank[half]]] + over, done="gru_first")
    first = pr.add("dve", lambda e: e.tensor_scalar(state[:, 0], c.condT[:].rearrange("p b k -> p k b"), c.h_scale[:], None, ALU.mult),
                   wait=over, done="gru_first")
    c.first_state = first
    for half in range(2):
        chunks = slice(2 * half, 2 * half + 2)
        hi = pr.add("dve", lambda e, half=half, chunks=chunks: e.tensor_copy(parts[0][half][:, :, 2], state[:, 0, chunks]),
                    wait=[first, cleared], done="gru_first")
        ready = pr.add("dve", lambda e, half=half, chunks=chunks: e.tensor_tensor(
            parts[0][half][:, :, 3], state[:, 0, chunks], parts[0][half][:, :, 2], ALU.subtract), wait=[hi], done="gru_first")

    registers = {}

    def load_register(e, name, source):
        registers[name] = e.alloc_register(f"act_{name}")
        e.reg_load(registers[name], source[0:1, 0:1].bitcast(INT32))

    pr.add("act", lambda e: load_register(e, "unscale", c.gate_unscale), wait=[c.scale])
    first_scale = mem.small("first_scale", 1)
    m = pr.add("dve", lambda e: e.tensor_tensor(first_scale[:], c.gate_scale[:], c.ih_unscale[:], ALU.mult), wait=[c.ih_scaled, c.scale], done="gru_first")
    pr.add("act", lambda e: load_register(e, "first_scale", first_scale), wait=[m])

    side_read = {6: c.bank_read[6], 7: c.bank_read[7]}
    side_count = [0]
    gates_made = {}
    gates_free = {}
    parts_read = {}

    def side_matmul(bank, lhs, rhs, k, wait, done=None):
        return pr.add("pe", lambda e: e.matmul(mem.bank(bank, P), lhs, rhs, start=(k == 0), stop=(k == GROUP - 1)),
                      wait=wait + [side_read[bank]], done=done)

    x_parts = mem.view("w_out", 0, FP16, 2, 2, NC, B * STEPS_PER_CHUNK)
    x_high, x_ready = {}, {}

    def split_inputs(q, k):
        source = c.xT[:, k, :, q * STEPS_PER_CHUNK:(q + 1) * STEPS_PER_CHUNK]
        high, low = (x_parts[:, q % 2, part, k].rearrange("p (b s) -> p b s", b=B) for part in range(2))
        hi = pr.add("act", lambda e: e.activation(high, source, ACT.Copy, scale=registers["x_scale"]),
                    wait=[x_scaled, parts_read.get(q)] + c.x2, done="x_high")
        x_ready[q] = pr.add("dve", lambda e: e.scalar_tensor_tensor(low, source, x_scale[:], high, ALU.mult, ALU.subtract), wait=[hi], done="x_low")

    def gate_group(q, j):
        bank = side_bank[side_count[0] % 2]
        side_count[0] += 1
        m, g, ch = j // 6, j % 6 // 2, j % 2
        block = g * NC + 2 * m + ch
        cols = slice(block * P, (block + 1) * P)
        for k in range(NC):
            if q == 0:
                made = side_matmul(bank, c.w_ih[:, k, cols], c.xT[:, k, :, :STEPS_PER_CHUNK], k, [c.w_ih16_done] + c.x2,
                                   "gates_in_sum" if k == NC - 1 else None)
            else:
                for part in range(4):
                    made = pr.add("pe", lambda e, k=k, part=part: e.matmul(
                        mem.bank(bank, P), c.w_ih16[:, part // 2, k, cols], x_parts[:, q % 2, part % 2, k],
                        start=(k == part == 0), stop=(k == part == NC - 1)), wait=[side_read[bank], x_ready[q], c.w_ih16_done],
                        done="gates_in_sum" if k == part == NC - 1 else None)
            if k == 1:
                yield None
        if q == 0:
            c.w_ih_read = made
        parts_read[q + 2] = made
        scale = "first_scale" if q == 0 else "gates_scale"

        def take():
            side_read[bank] = gates_made[q] = pr.add("act", lambda e: e.activation(
                gates_in[:, q % 2, j], mem.bank(bank, B, STEPS_PER_CHUNK), ACT.Identity, scale=registers[scale],
                bias=bias_in[:, m, g, ch:ch + 1]), wait=[made, bi] + gates_free.get(q, []), done="gates_in")
        yield take

    rows_read = [None] * 4
    rows_count = [0]
    x3_made = {}

    def rows_group(tile, b, quarter):
        bank = side_bank[side_count[0] % 2]
        side_count[0] += 1
        slot = rows_count[0] // 4 % 4
        rows_count[0] += 1
        cols = slice(quarter * P, (quarter + 1) * P)
        for k in range(NC):
            made = side_matmul(bank, c.xT[:, k, b, tile * P:(tile + 1) * P], c.sampling[:, b, k, cols], k,
                               [x3_made[tile, b], c.sampling_done[b]], "rows_sum" if k == NC - 1 else None)
            if k == 1:
                yield None
        def take():
            side_read[bank] = taken = pr.add("act", lambda e: e.activation(rows_out[:, slot, cols], mem.bank(bank, P), ACT.Copy),
                                             wait=[made, rows_read[slot], c.sampling_done[B - 1]], done="rows_out")
            if quarter == 3:
                rows_read[slot] = c.out_event = pr.dma("sp", out[b, tile * P:(tile + 1) * P], rows_out[:, slot], f"out{slot}", wait=[taken])
        yield take

    for j in range(12):
        for item in gate_group(0, j):
            if item:
                item()

    xm = mem.small("x_most_all", 1)
    m = pr.add("dve", lambda e: e.tensor_reduce(xm[:], c.x_most[:], AX.X, ALU.max), wait=[c.x_most_done], done="x_most")
    x_scale, x_unscale, x_scaled = scale_of(pr, mem, "x", xm[:], m, "x_scale")
    gates_scale = mem.small("gates_scale", 1)
    m = pr.add("dve", lambda e: e.tensor_tensor(gates_scale[:], x_unscale[:], c.ih_unscale[:], ALU.mult), wait=[x_scaled], done="x_scale")
    m = pr.add("dve", lambda e: e.tensor_scalar(gates_scale[:], gates_scale[:], c.gate_scale[:], None, ALU.mult), wait=[m], done="x_scale")
    pr.add("act", lambda e: load_register(e, "x_scale", x_scale), wait=[m])
    pr.add("act", lambda e: load_register(e, "gates_scale", gates_scale), wait=[m])
    for k in range(NC):
        split_inputs(1, k)

    def add_states(tile, b, k, ready):
        x3_made[tile, b] = pr.add("dve", lambda e: e.scalar_tensor_tensor(
            c.xT[:, k, b, tile * P:(tile + 1) * P], state[:, 1 + tile * P:1 + (tile + 1) * P, k, b], c.h_unscale[:],
            c.xT[:, k, b, tile * P:(tile + 1) * P], ALU.mult, ALU.add), wait=ready, done="x3")

    rs_read, zs_read, nm_read, nsum_read = [c.bank_read[i] for i in (0, 1)], [c.bank_read[i] for i in (2, 3)], \
        [c.bank_read[i] for i in (4, 5)], [None, None]
    parts_ready = [[ready], [ready]]
    at = {u: i for i, u in enumerate(UNITS)}
    last_unit = {(h, g): max((k + "AB"[h] + g for k in "AB"), key=at.get) for h in range(2) for g in "rzn"}
    side, groups = None, []
    add_queue = []
    h_last = None
    put = {}
    z_put = any(x.startswith("zput") for x in ORDER)

    def put_gate(s, half, g):
        if s == S:
            return
        q, ss = s // STEPS_PER_CHUNK, s % STEPS_PER_CHUNK
        source = gates_in[:, q % 2, 6 * half + 2 * g:6 * half + 2 * g + 2, :, ss]
        if g == 2:
            put[half, g] = pr.add("pool", lambda e: e.tensor_copy(nm[half][:, :, 5], source),
                                  wait=[gates_made[q], nsum_read[half]], done=f"n_in{half}")
        else:
            put[half, g] = pr.add("act", lambda e: e.activation(of_bank((r_bank, z_bank)[g][half])[:, :, 4], source, ACT.Copy),
                                  wait=[gates_made[q], (rs_read, zs_read)[g][half]], done=f"{'rz'[g]}_in{half}")

    for half in range(2):
        for g in ((0, 1, 2) if z_put else (0, 2)):
            put_gate(0, half, g)
    ev = {}
    for s in range(S):
        q, ss, now, nxt = s // STEPS_PER_CHUNK, s % STEPS_PER_CHUNK, s % 2, (s + 1) % 2
        gi = gates_in[:, q % 2, :, :, ss]
        summed, started = {}, set()
        for u in UNITS:
            read, half, g = "AB".index(u[0]), "AB".index(u[1]), "rzn".index(u[2])
            bank = (r_bank, z_bank, n_bank)[g][half]
            for ch in range(2):
                for k in range(2):
                    for part in range(2):
                        start = (half, g) not in started
                        started.add((half, g))
                        final = last_unit[half, u[2]] == u and ch == k == part == 1
                        product = pr.add("pe", lambda e, bank=bank, ch=ch, part=part, k=k, read=read, j=6 * half + 2 * g + ch, now=now, start=start: e.matmul(
                            mem.bank(bank, 2, 5 * B)[:, ch, :4 * B], c.w16[:, part, 2 * read + k, j], parts[now][read][:, k].rearrange("p q b -> p (q b)"),
                            start=start, stop=(read == 1), skip_group_check=True),
                            wait=parts_ready[read] + ([(rs_read, zs_read, nm_read)[g][half], put.get((half, g))] if start and g < 2 else [nm_read[half]] if start else []) + [c.w16_done], done=f"{u[2]}_products{u[1]}" if final else None)
                        if final:
                            summed[half, u[2]] = product
        if ss == 0:
            assert side is None and not groups
            if q + 1 < S // STEPS_PER_CHUNK:
                gate_groups = [lambda j=j, q=q: gate_group(q + 1, j) for j in range(12)]
            else:
                gate_groups = []
            rows_groups = []
            for i in range(4):
                index = (s - P) // 8 + i
                if index >= 0:
                    rows_groups.append(lambda index=index: rows_group(index // 16, index % 16 // 4, index % 4))
            for i in range(4):
                groups += gate_groups[3 * i:3 * i + 3] + rows_groups[i:i + 1]
            gates_free[q + 1] = list(put.values()) + [ev.get(("zadd", h)) for h in range(2)] if s else []
        takes = []
        if side is None and groups:
            side = groups.pop(0)()
        if side is not None:
            item = next(side)
            if item is not None:
                takes.append(item)
                side = None

        ev = {}
        h_before = [c.first_state, c.first_state] if s == 0 else h_before
        for name in ORDER:
            op, half = name[:-1], "AB".index(name[-1])
            chunks = slice(2 * half, 2 * half + 2)
            key = lambda n: ev[n, half]

            def add(engine, emit, *wait, op=op, half=half):
                ev[op, half] = pr.add(engine, emit, wait=list(wait), done=f"{op}{half}")
                return ev[op, half]

            if op == "rsum":
                rs_read[half] = add("dve", lambda e, half=half: e.tensor_reduce(
                    rz[half][:, 0:2], of_bank(r_bank[half]).rearrange("p c q b -> p c b q"), AX.X, ALU.add), summed[half, "r"], put[half, 0])
            elif op == "zsum":
                zs_read[half] = add("dve", lambda e, half=half: e.tensor_reduce(
                    rz[half][:, 2:4], of_bank(z_bank[half])[:, :, :5 if z_put else 4].rearrange("p c q b -> p c b q"), AX.X, ALU.add),
                    summed[half, "z"], put.get((half, 1)))
            elif op == "zadd":
                add("dve", lambda e, half=half, gi=gi: e.tensor_tensor(rz[half][:, 2:4], rz[half][:, 2:4], gi[:, 6 * half + 2:6 * half + 4], ALU.add),
                    key("zsum"))
            elif op == "rsig":
                add("act", lambda e, half=half: e.activation(gate[half][:, 0:2], rz[half][:, 0:2], ACT.Sigmoid, scale=registers["unscale"]),
                    key("rsum"))
            elif op == "zsig":
                add("act", lambda e, half=half: e.activation(gate[half][:, 2:4], rz[half][:, 2:4], ACT.Sigmoid, scale=registers["unscale"]),
                    key("zsum" if z_put else "zadd"))
            elif op == "nmul":
                nm_read[half] = add("dve", lambda e, half=half: e.tensor_tensor(
                    nm[half][:, :, 0:5], of_bank(n_bank[half]), gate[half][:, 0:2].unsqueeze(2).broadcast_to([P, 2, 5, B]), ALU.mult),
                    summed[half, "n"], key("rsig"))
            elif op == "nsum":
                nsum_read[half] = add("dve", lambda e, half=half: e.tensor_reduce(
                    nsum[half][:], nm[half][:].rearrange("p c q b -> p c b q"), AX.X, ALU.add), key("nmul"), put[half, 2])
            elif op == "tanh":
                add("act", lambda e, half=half: e.activation(new[half][:], nsum[half][:], ACT.Tanh, scale=registers["unscale"]), key("nsum"))
            elif op == "omz":
                add("dve", lambda e, half=half: e.tensor_scalar(one_minus_z[half][:], gate[half][:, 2:4], 1.0, c.minus_h_scale[:],
                                                               ALU.subtract, ALU.mult), key("zsig"))
            elif op == "zh":
                add("dve", lambda e, half=half, chunks=chunks, s=s: e.tensor_tensor(zh[half][:], gate[half][:, 2:4], state[:, s, chunks], ALU.mult),
                    key("zsig"), h_before[half])
            elif op == "zsplit":
                add("act", lambda e, half=half, nxt=nxt: e.activation(parts[nxt][half][:, :, 2], zh[half][:], ACT.Copy), key("zh"))
            elif op == "zlow":
                add("pool", lambda e, half=half, nxt=nxt: e.tensor_tensor(parts[nxt][half][:, :, 3], zh[half][:], parts[nxt][half][:, :, 2],
                                                                         ALU.subtract), key("zsplit"), key("zh"))
            elif op == "tmul":
                t_f = add("dve", lambda e, half=half: e.tensor_tensor(t_[half][:], new[half][:], one_minus_z[half][:], ALU.mult),
                          key("tanh"), key("omz"), h_before[half])
                ev["t16", half] = pr.add("dve", lambda e, half=half, nxt=nxt: e.tensor_tensor(
                    parts[nxt][half][:, :, 0], new[half][:], one_minus_z[half][:], ALU.mult), done=f"t16{half}")
            elif op == "tlow":
                add("dve", lambda e, half=half, nxt=nxt: e.tensor_tensor(parts[nxt][half][:, :, 1], t_[half][:], parts[nxt][half][:, :, 0],
                                                                        ALU.subtract), key("tmul"), key("t16"))
            elif op in ("rput", "zput", "nput"):
                put_gate(s + 1, half, "rzn".index(op[0]))
            elif op == "state":
                ev["state", half] = pr.add("pool", lambda e, half=half, chunks=chunks, s=s: e.tensor_tensor(
                    state[:, s + 1, chunks], t_[half][:], zh[half][:], ALU.add), wait=[key("tmul"), key("zh")], done="state")
        parts_ready = [[ev["zlow", h], ev["tlow", h], ev["zsplit", h]] for h in range(2)]
        h_before = [ev["state", h] for h in range(2)]
        for take in takes:
            take()
        if 26 <= ss < 26 + NC and q + 2 < S // STEPS_PER_CHUNK:
            split_inputs(q + 2, ss - 26)
        if (s + 1) % P == 0:
            add_queue += [(s // P, b, k) for b in range(B) for k in range(NC)]
        if jobs:
            jobs.pop(0)()
        if add_queue and s + 1 < S:
            add_states(*add_queue.pop(0), [ev["state", 1]])
        c.state_done = ev["state", 1]
    return dict(state=state, add_states=add_states, add_queue=add_queue, x3_made=x3_made, rows_out=rows_out, rows_read=rows_read)


def last_tile(pr, mem, c, left, out):
    tile = NT - 1
    while left["add_queue"]:
        left["add_states"](*left["add_queue"].pop(0), [c.state_done])
    events = []
    for b in range(B):
        for k in range(NC):
            made = pr.add("pe", lambda e, b=b, k=k: e.matmul(mem.bank(b, D), c.xT[:, k, b, tile * P:(tile + 1) * P], c.sampling[:, b, k],
                                                            start=(k == 0), stop=(k == NC - 1)),
                          wait=[left["x3_made"][tile, b], c.sampling_done[b]], done="last_rows" if k == NC - 1 else None)
        slot = b
        engine = ("act", "dve")[b % 2]
        emit = (lambda e, b=b, slot=slot: e.activation(left["rows_out"][:, slot], mem.bank(b, D), ACT.Copy)) if engine == "act" else \
            (lambda e, b=b, slot=slot: e.tensor_copy(left["rows_out"][:, slot], mem.bank(b, D)))
        taken = pr.add(engine, emit, wait=[made, left["rows_read"][slot]], done=f"last_taken_{engine}")
        events.append(pr.dma("sp", out[b, tile * P:(tile + 1) * P], left["rows_out"][:, slot], f"out{slot}", wait=[taken]))
    pr.add("sp", None, wait=events)


_INS = ["x", "fside_BxSx1_0", "cond_2048", "L1_cond_W_emb", "L1_cond_b_emb", "L1_cond_g_norm", "L1_cond_W_qkv", "L1_cond_g_q",
        "L1_cond_g_k", "L1_cond_W_out", "L2_cond_W_ih", "L2_cond_W_hh", "L2_cond_b_ih", "L2_cond_b_hh"]


def kernel(**inputs):
    import numpy as _np
    import concourse.bacc as _bacc
    from concourse import mybir as _mybir
    from concourse.bass_utils import run_bass_kernel_spmd as _run

    nc = _bacc.Bacc("TRN2", target_bir_lowering=False, num_devices=1)
    arrays, args = {}, []
    for name in _INS:
        a = _np.ascontiguousarray(inputs[name])
        arrays[f"in_{name}_dram"] = a
        args.append(nc.dram_tensor(f"in_{name}_dram", a.shape, _mybir.dt.from_np(a.dtype), kind="ExternalInput").ap())
    out = nc.dram_tensor("out_dram", (B, S, D), FP32, kind="ExternalOutput").ap()
    build(nc, *args, out)
    r = _run(nc, [arrays], core_ids=[0])
    return r.results[0]["out_dram"]
```
